# Optimizing a Trainium2 kernel written in Bass

```python
import numpy as np
import jax
import jax.numpy as jnp

def _softmax(x, axis=-1):
    return jax.nn.softmax(x, axis=axis)
def _gelu(x):
    return jax.nn.gelu(x, approximate=True)
def _silu(x):
    return jax.nn.silu(x)
def _sigmoid(x):
    return jax.nn.sigmoid(x)
def _layernorm(x, axis=-1, eps=1e-5):
    m = jnp.mean(x, axis=axis, keepdims=True)
    v = jnp.var(x, axis=axis, keepdims=True)
    return (x - m) / jnp.sqrt(v + eps)
def _scatter_add(tgt, idx, src, axis=0):
    return tgt.at[idx].add(src)
def _segment_sum(src, seg, n):
    return jax.ops.segment_sum(src, seg, n)

kernel_name = 'mk_dlrm_tower_d1_rec_992d95'

def setup_inputs(seed: int = 0):
    np.random.seed(seed)
    _w = jnp.asarray
    def _rec_inputs():
        import jax
        import jax.numpy as jnp
        _tk = jax.random.key(seed)
        dense_ctx = jax.random.normal(jax.random.fold_in(_tk, 190), (1024, 16), jnp.float32)
        ids = jnp.stack([jax.random.randint(jax.random.fold_in(_tk, 200 + f), (1024,), 0, v, jnp.int32) for f, v in enumerate([1000, 10000, 1000, 1000, 100000, 10000, 1000, 1000, 10000, 1000, 100000, 1000, 10000, 10000, 1000, 1000000, 10000, 10000, 100000, 10000, 1000, 100000, 1000000, 1000000, 10000, 1000, 100000, 1000, 1000, 1000, 10000, 1000, 10000, 1000, 10000, 100000, 10000, 1000, 1000])], axis=1)
        tbl_0 = 0.05 * jax.random.normal(jax.random.fold_in(_tk, 500 + 0), (1000, 16), jnp.float32)
        tbl_1 = 0.05 * jax.random.normal(jax.random.fold_in(_tk, 500 + 1), (10000, 16), jnp.float32)
        tbl_2 = 0.05 * jax.random.normal(jax.random.fold_in(_tk, 500 + 2), (1000, 16), jnp.float32)
        tbl_3 = 0.05 * jax.random.normal(jax.random.fold_in(_tk, 500 + 3), (1000, 16), jnp.float32)
        tbl_4 = 0.05 * jax.random.normal(jax.random.fold_in(_tk, 500 + 4), (100000, 16), jnp.float32)
        tbl_5 = 0.05 * jax.random.normal(jax.random.fold_in(_tk, 500 + 5), (10000, 16), jnp.float32)
        tbl_6 = 0.05 * jax.random.normal(jax.random.fold_in(_tk, 500 + 6), (1000, 16), jnp.float32)
        tbl_7 = 0.05 * jax.random.normal(jax.random.fold_in(_tk, 500 + 7), (1000, 16), jnp.float32)
        tbl_8 = 0.05 * jax.random.normal(jax.random.fold_in(_tk, 500 + 8), (10000, 16), jnp.float32)
        tbl_9 = 0.05 * jax.random.normal(jax.random.fold_in(_tk, 500 + 9), (1000, 16), jnp.float32)
        tbl_10 = 0.05 * jax.random.normal(jax.random.fold_in(_tk, 500 + 10), (100000, 16), jnp.float32)
        tbl_11 = 0.05 * jax.random.normal(jax.random.fold_in(_tk, 500 + 11), (1000, 16), jnp.float32)
        tbl_12 = 0.05 * jax.random.normal(jax.random.fold_in(_tk, 500 + 12), (10000, 16), jnp.float32)
        tbl_13 = 0.05 * jax.random.normal(jax.random.fold_in(_tk, 500 + 13), (10000, 16), jnp.float32)
        tbl_14 = 0.05 * jax.random.normal(jax.random.fold_in(_tk, 500 + 14), (1000, 16), jnp.float32)
        tbl_15 = 0.05 * jax.random.normal(jax.random.fold_in(_tk, 500 + 15), (1000000, 16), jnp.float32)
        tbl_16 = 0.05 * jax.random.normal(jax.random.fold_in(_tk, 500 + 16), (10000, 16), jnp.float32)
        tbl_17 = 0.05 * jax.random.normal(jax.random.fold_in(_tk, 500 + 17), (10000, 16), jnp.float32)
        tbl_18 = 0.05 * jax.random.normal(jax.random.fold_in(_tk, 500 + 18), (100000, 16), jnp.float32)
        tbl_19 = 0.05 * jax.random.normal(jax.random.fold_in(_tk, 500 + 19), (10000, 16), jnp.float32)
        tbl_20 = 0.05 * jax.random.normal(jax.random.fold_in(_tk, 500 + 20), (1000, 16), jnp.float32)
        tbl_21 = 0.05 * jax.random.normal(jax.random.fold_in(_tk, 500 + 21), (100000, 16), jnp.float32)
        tbl_22 = 0.05 * jax.random.normal(jax.random.fold_in(_tk, 500 + 22), (1000000, 16), jnp.float32)
        tbl_23 = 0.05 * jax.random.normal(jax.random.fold_in(_tk, 500 + 23), (1000000, 16), jnp.float32)
        tbl_24 = 0.05 * jax.random.normal(jax.random.fold_in(_tk, 500 + 24), (10000, 16), jnp.float32)
        tbl_25 = 0.05 * jax.random.normal(jax.random.fold_in(_tk, 500 + 25), (1000, 16), jnp.float32)
        tbl_26 = 0.05 * jax.random.normal(jax.random.fold_in(_tk, 500 + 26), (100000, 16), jnp.float32)
        tbl_27 = 0.05 * jax.random.normal(jax.random.fold_in(_tk, 500 + 27), (1000, 16), jnp.float32)
        tbl_28 = 0.05 * jax.random.normal(jax.random.fold_in(_tk, 500 + 28), (1000, 16), jnp.float32)
        tbl_29 = 0.05 * jax.random.normal(jax.random.fold_in(_tk, 500 + 29), (1000, 16), jnp.float32)
        tbl_30 = 0.05 * jax.random.normal(jax.random.fold_in(_tk, 500 + 30), (10000, 16), jnp.float32)
        tbl_31 = 0.05 * jax.random.normal(jax.random.fold_in(_tk, 500 + 31), (1000, 16), jnp.float32)
        tbl_32 = 0.05 * jax.random.normal(jax.random.fold_in(_tk, 500 + 32), (10000, 16), jnp.float32)
        tbl_33 = 0.05 * jax.random.normal(jax.random.fold_in(_tk, 500 + 33), (1000, 16), jnp.float32)
        tbl_34 = 0.05 * jax.random.normal(jax.random.fold_in(_tk, 500 + 34), (10000, 16), jnp.float32)
        tbl_35 = 0.05 * jax.random.normal(jax.random.fold_in(_tk, 500 + 35), (100000, 16), jnp.float32)
        tbl_36 = 0.05 * jax.random.normal(jax.random.fold_in(_tk, 500 + 36), (10000, 16), jnp.float32)
        tbl_37 = 0.05 * jax.random.normal(jax.random.fold_in(_tk, 500 + 37), (1000, 16), jnp.float32)
        tbl_38 = 0.05 * jax.random.normal(jax.random.fold_in(_tk, 500 + 38), (1000, 16), jnp.float32)
        _rk = jax.random.fold_in(_tk, 7)
        W_top1 = 0.05 * jax.random.normal(jax.random.fold_in(_tk, 801), (400, 512), jnp.float32)
        W_top2 = 0.0441942 * jax.random.normal(jax.random.fold_in(_tk, 802), (512, 256), jnp.float32)
        W_top3 = 0.0625 * jax.random.normal(jax.random.fold_in(_tk, 803), (256, 1), jnp.float32)
        b_top1 = jnp.zeros((512,), jnp.float32)
        b_top2 = jnp.zeros((256,), jnp.float32)
        return dense_ctx, ids, tbl_0, tbl_1, tbl_2, tbl_3, tbl_4, tbl_5, tbl_6, tbl_7, tbl_8, tbl_9, tbl_10, tbl_11, tbl_12, tbl_13, tbl_14, tbl_15, tbl_16, tbl_17, tbl_18, tbl_19, tbl_20, tbl_21, tbl_22, tbl_23, tbl_24, tbl_25, tbl_26, tbl_27, tbl_28, tbl_29, tbl_30, tbl_31, tbl_32, tbl_33, tbl_34, tbl_35, tbl_36, tbl_37, tbl_38, W_top1, b_top1, W_top2, b_top2, W_top3
    dense_ctx, ids, tbl_0, tbl_1, tbl_2, tbl_3, tbl_4, tbl_5, tbl_6, tbl_7, tbl_8, tbl_9, tbl_10, tbl_11, tbl_12, tbl_13, tbl_14, tbl_15, tbl_16, tbl_17, tbl_18, tbl_19, tbl_20, tbl_21, tbl_22, tbl_23, tbl_24, tbl_25, tbl_26, tbl_27, tbl_28, tbl_29, tbl_30, tbl_31, tbl_32, tbl_33, tbl_34, tbl_35, tbl_36, tbl_37, tbl_38, W_top1, b_top1, W_top2, b_top2, W_top3 = _rec_inputs()
    def _L0_rec_setup():
        import jax, jax.numpy as jnp
        import numpy as np
        B, F0, D = (2048, 39, 16)
        CROSS = [128, 128, 128]
        key = jax.random.key(seed)
        k0, k1, k2, k3 = jax.random.split(key, 4)
        inputs = jax.random.normal(k0, (B, F0, D), dtype=jnp.float32)
        f0 = jax.random.normal(k1, (F0 * F0, CROSS[0]), dtype=jnp.float32) * 0.05
        f1 = jax.random.normal(k2, (CROSS[0] * F0, CROSS[1]), dtype=jnp.float32) * 0.05
        f2 = jax.random.normal(k3, (CROSS[1] * F0, CROSS[2]), dtype=jnp.float32) * 0.05
        return {'inputs': inputs, 'f0': f0, 'f1': f1, 'f2': f2}
    _L0_rec_all = _L0_rec_setup()
    _L0_rec_in = {k: v for k, v in _L0_rec_all.items() if k in ('f0', 'f1', 'f2', )}
    del _L0_rec_all

    return {
        "dense_ctx": dense_ctx,
        "ids": ids,
        "tbl_0": tbl_0,
        "tbl_1": tbl_1,
        "tbl_2": tbl_2,
        "tbl_3": tbl_3,
        "tbl_4": tbl_4,
        "tbl_5": tbl_5,
        "tbl_6": tbl_6,
        "tbl_7": tbl_7,
        "tbl_8": tbl_8,
        "tbl_9": tbl_9,
        "tbl_10": tbl_10,
        "tbl_11": tbl_11,
        "tbl_12": tbl_12,
        "tbl_13": tbl_13,
        "tbl_14": tbl_14,
        "tbl_15": tbl_15,
        "tbl_16": tbl_16,
        "tbl_17": tbl_17,
        "tbl_18": tbl_18,
        "tbl_19": tbl_19,
        "tbl_20": tbl_20,
        "tbl_21": tbl_21,
        "tbl_22": tbl_22,
        "tbl_23": tbl_23,
        "tbl_24": tbl_24,
        "tbl_25": tbl_25,
        "tbl_26": tbl_26,
        "tbl_27": tbl_27,
        "tbl_28": tbl_28,
        "tbl_29": tbl_29,
        "tbl_30": tbl_30,
        "tbl_31": tbl_31,
        "tbl_32": tbl_32,
        "tbl_33": tbl_33,
        "tbl_34": tbl_34,
        "tbl_35": tbl_35,
        "tbl_36": tbl_36,
        "tbl_37": tbl_37,
        "tbl_38": tbl_38,
        "W_top1": W_top1,
        "b_top1": b_top1,
        "W_top2": W_top2,
        "b_top2": b_top2,
        "W_top3": W_top3,
        "L0_rec_f0": _L0_rec_in["f0"],
        "L0_rec_f1": _L0_rec_in["f1"],
        "L0_rec_f2": _L0_rec_in["f2"],
    }

def reference(dense_ctx, ids, tbl_0, tbl_1, tbl_2, tbl_3, tbl_4, tbl_5, tbl_6, tbl_7, tbl_8, tbl_9, tbl_10, tbl_11, tbl_12, tbl_13, tbl_14, tbl_15, tbl_16, tbl_17, tbl_18, tbl_19, tbl_20, tbl_21, tbl_22, tbl_23, tbl_24, tbl_25, tbl_26, tbl_27, tbl_28, tbl_29, tbl_30, tbl_31, tbl_32, tbl_33, tbl_34, tbl_35, tbl_36, tbl_37, tbl_38, W_top1, b_top1, W_top2, b_top2, W_top3, L0_rec_f0, L0_rec_f1, L0_rec_f2):
    import jax
    import jax.numpy as jnp
    def _L0_rec_ref(inputs, f0, f1, f2):
        import jax, jax.numpy as jnp
        import numpy as np
        B, F0, D = (2048, 39, 16)
        CROSS = [128, 128, 128]
        filters = [f0, f1, f2]
        x0 = inputs
        xk = inputs
        outs = []
        for W in filters:
            b, f, d = x0.shape
            g = xk.shape[1]
            z = jnp.einsum('bfd,bgd->bfgd', x0, xk).reshape(b, f * g, d)
            cur = jnp.einsum('bpd,pm->bmd', z, W)
            outs.append(cur)
            xk = cur
        result = jnp.concatenate(outs, axis=1)
        return jnp.sum(result, axis=-1)

    e = jnp.stack([tbl_0[ids[:, 0]], tbl_1[ids[:, 1]], tbl_2[ids[:, 2]], tbl_3[ids[:, 3]], tbl_4[ids[:, 4]], tbl_5[ids[:, 5]], tbl_6[ids[:, 6]], tbl_7[ids[:, 7]], tbl_8[ids[:, 8]], tbl_9[ids[:, 9]], tbl_10[ids[:, 10]], tbl_11[ids[:, 11]], tbl_12[ids[:, 12]], tbl_13[ids[:, 13]], tbl_14[ids[:, 14]], tbl_15[ids[:, 15]], tbl_16[ids[:, 16]], tbl_17[ids[:, 17]], tbl_18[ids[:, 18]], tbl_19[ids[:, 19]], tbl_20[ids[:, 20]], tbl_21[ids[:, 21]], tbl_22[ids[:, 22]], tbl_23[ids[:, 23]], tbl_24[ids[:, 24]], tbl_25[ids[:, 25]], tbl_26[ids[:, 26]], tbl_27[ids[:, 27]], tbl_28[ids[:, 28]], tbl_29[ids[:, 29]], tbl_30[ids[:, 30]], tbl_31[ids[:, 31]], tbl_32[ids[:, 32]], tbl_33[ids[:, 33]], tbl_34[ids[:, 34]], tbl_35[ids[:, 35]], tbl_36[ids[:, 36]], tbl_37[ids[:, 37]], tbl_38[ids[:, 38]]], axis=1)
    z = _L0_rec_ref(e, L0_rec_f0, L0_rec_f1, L0_rec_f2)
    z = z.reshape(z.shape[0], -1)
    h = jnp.concatenate([z, dense_ctx], axis=1)
    h = jnp.maximum(h @ W_top1 + b_top1, 0.0)
    h = jnp.maximum(h @ W_top2 + b_top2, 0.0)
    y = h @ W_top3
    return y


_drawn_inputs = setup_inputs


def setup_inputs(seed=0):
    import zlib

    import numpy as np

    out = dict(_drawn_inputs(seed))
    spreads = {'b_top1': (0.0, 0.58), 'b_top2': (0.0, 0.1)}
    factors = {'tbl_0': 4.516,
     'tbl_1': 4.999,
     'tbl_2': 4.693,
     'tbl_3': 4.916,
     'tbl_4': 4.757,
     'tbl_5': 4.999,
     'tbl_6': 4.606,
     'tbl_7': 4.587,
     'tbl_8': 4.826,
     'tbl_9': 4.471,
     'tbl_10': 5.053,
     'tbl_11': 4.51,
     'tbl_12': 4.224,
     'tbl_13': 4.369,
     'tbl_14': 4.379,
     'tbl_15': 4.855,
     'tbl_16': 5.113,
     'tbl_17': 4.827,
     'tbl_18': 4.889,
     'tbl_19': 4.881,
     'tbl_20': 4.695,
     'tbl_21': 4.618,
     'tbl_22': 4.557,
     'tbl_23': 4.727,
     'tbl_24': 4.594,
     'tbl_25': 4.59,
     'tbl_26': 5.016,
     'tbl_27': 4.993,
     'tbl_28': 4.785,
     'tbl_29': 4.653,
     'tbl_30': 4.682,
     'tbl_31': 4.327,
     'tbl_32': 4.627,
     'tbl_33': 4.769,
     'tbl_34': 4.472,
     'tbl_35': 4.431,
     'tbl_36': 4.964,
     'tbl_37': 4.765,
     'tbl_38': 5.022,
     'L0_rec_f1': 5.212,
     'L0_rec_f2': 8.0}
    for name, (base, spread) in spreads.items():
        noise = np.random.default_rng([zlib.crc32(name.encode()), seed]).standard_normal(out[name].shape)
        drawn = base * np.exp(spread * noise) if base else spread * noise
        out[name] = jnp.asarray(drawn.astype(out[name].dtype))
    for name, factor in factors.items():
        out[name] = (out[name] * factor).astype(out[name].dtype)
    return out
```

```python
from contextlib import ExitStack

import numpy as np

import concourse.bass as bass
from concourse import mybir

F32 = mybir.dt.float32
F32R = mybir.dt.float32r
I32 = mybir.dt.int32
U32 = mybir.dt.uint32
ALU = mybir.AluOpType
ACT = mybir.ActivationFunctionType
AX = mybir.AxisListType

BATCH = 1024
NF = 39
D = 16
M = 128
DENSE = 16
H1, H2 = 512, 256

P = 128
FP = NF + 1
CHUNK_B = P // D
QUAD = 4
COLS = QUAD * P
QUAD_B = QUAD * CHUNK_B
QUADS = BATCH // QUAD_B
TILES = BATCH // P
TILE_QUADS = QUADS // TILES
TILE_CHUNKS = TILE_QUADS * QUAD
CHUNKS = QUADS * QUAD

SHIFTS = (NF + 1) // 2
BLOCK_SHIFTS = 3
BLOCKS = -(-SHIFTS // BLOCK_SHIFTS)

GF = 4
GROUPS = -(-NF // GF)
GROUP_F = [min(GF, NF - GF * j) for j in range(GROUPS)]
POSITIONS = QUAD * GROUPS
DVE_F = sum(GROUP_F[0::2])
ACT_F = sum(GROUP_F[1::2])
ACT_GROUPS = GROUPS // 2
Y_BANKS = 4

PE_TRANSPOSE, PE_REP = 9, 12
PE_SHIFT = [13, 16, 17, 19, 21, 24, 26]
PE_W0 = [17, 20, 23, 24, 26, 31, 32]
ACT_XSPLIT, ACT_XT, ACT_REP, ACT_CUR0_LO, ACT_CUR0_HI = 3, 9, 11, 31, 1
DVE_XSPLIT, DVE_CUR0_LO, DVE_CROSS0, DVE_CUR0_HI = 4, 34, 38, 2
DVE_PAIRS = [14, 16, 18, 20, 24, 26, 28]
PE_GRAM = 5
ACT_GRAM = 9
DVE_FOLD = (4, 6, 8)
LO = 3 * P
GATHERS_A_CHUNK = 4


def dve_done(q, pos):
    return q * (QUAD * DVE_F) + GF * (pos // 2 + 1)


def act_done(q, pos):
    return q * (QUAD * ACT_F) + ACT_F * (pos // GROUPS) + min(GF * ((pos % GROUPS) // 2 + 1), ACT_F)


def build(nc, dense, ids, tables, w_top1, b_top1, w_top2, b_top2, w_top3, w0_pair, w0_twin, f1, f2,
          selectors, identity, out):
    scratch = nc.dram_tensor("x0_by_column", [BATCH * D, FP], F32, kind="Internal").ap()
    scratch_tiles = scratch.rearrange("(b d) f -> b (d f)", d=D)
    scratch_chunks = scratch.rearrange("(n p) f -> p n f", p=P)

    with ExitStack() as ctx:
        def sb(name, shape, dt=F32):
            return ctx.enter_context(nc.sbuf_tensor(name, shape, dt))

        def psum(name, shape):
            return ctx.enter_context(nc.psum_tensor(name, shape, F32))

        def sem(name):
            return ctx.enter_context(nc.semaphore(name))

        w1_hi = sb("w1_hi", [P, NF * M], F32R)
        w1_lo = sb("w1_lo", [P, NF * M], F32R)
        w2_sb = sb("w2_sb", [P, NF * M])
        w0_sym = sb("w0_sym", [P, BLOCKS, M])
        sel = sb("sel", [P, BLOCKS + 1, P], F32R)
        ident = sb("ident", [P, P])
        wt1 = sb("wt1", [P, 4, H1])
        wt2 = sb("wt2", [P, H1 // P, H2])
        wt3 = sb("wt3", [P, H2 // P])
        bt1 = sb("bt1", [P, H1 // P])
        bt2 = sb("bt2", [P, H2 // P])
        ids_sb = sb("ids_sb", [P, NF], I32)
        gathered_x = sb("gathered_x", [P, NF, D])
        permuted_x = sb("permuted_x", [P, D, FP])
        x_next = sb("x_next", [P, QUAD, FP])
        x_dve = sb("x_dve", [P, QUAD, FP])
        x_act = sb("x_act", [P, QUAD, FP])
        x_diag = sb("x_diag", [P, 2, QUAD, CHUNK_B * FP])
        x_split = sb("x_split", [P, QUAD, P], F32R)
        xT = sb("xT", [P, COLS], F32R)
        rep = sb("rep", [P, COLS])
        pairs = sb("pairs", [P, 3, COLS])
        cur0_hi = sb("cur0_hi", [P, COLS], F32R)
        cur0_lo = sb("cur0_lo", [P, COLS], F32R)
        scaled = sb("scaled", [P, 2, ACT_GROUPS, GF * M])
        acc = sb("acc", [P, 2, 2 * M])
        fold = sb("fold", [P, 2, 2 * M])
        cur1 = sb("cur1", [P, 2, M])
        gram = sb("gram", [P, FP, 2 * P])
        cross0T = sb("cross0T", [P, BATCH])
        cross1T = sb("cross1T", [P, BATCH])
        cross2T = sb("cross2T", [P, BATCH])
        denseT = sb("denseT", [P, BATCH])
        dense_sb = sb("dense_sb", [P, TILES, P])
        y_sb = sb("y_sb", [1, BATCH])

        stage = gram[:, :, :].rearrange("p f b -> p (f b)")
        f1_stage = stage[:, 0:NF * M]
        o = NF * M
        sel_stage = stage[:, o:o + (BLOCKS + 1) * P].rearrange("p (j r) -> p j r", r=P)
        o += (BLOCKS + 1) * P
        pair_stage = stage[:, o:o + BLOCKS * M].rearrange("p (j m) -> p j m", m=M)
        o += BLOCKS * M
        twin_stage = stage[:, o:o + BLOCKS * M].rearrange("p (j m) -> p j m", m=M)
        h1T = scaled[:, 0, 0:H1 // P, :]
        h2T = scaled[:, 1, 0:H2 // P, :]

        y_ps = psum("y_ps", [P, Y_BANKS, 512])
        sel_ps = psum("sel_ps", [P, 2, 512])
        cur0_ps = psum("cur0_ps", [P, 512])
        gram_ps = psum("gram_ps", [P, 512])

        s_ids = sem("s_ids")
        s_gathered = sem("s_gathered")
        s_permuted = sem("s_permuted")
        s_scratch = sem("s_scratch")
        s_x = sem("s_x")
        s_diag = sem("s_diag")
        s_sel_in = sem("s_sel_in")
        s_w0_in = sem("s_w0_in")
        s_f1_in = sem("s_f1_in")
        s_rest_in = sem("s_rest_in")
        s_dense_in = sem("s_dense_in")
        s_out = sem("s_out")
        s_zero = sem("s_zero")
        s_zeroD = sem("s_zeroD")
        s_sel = sem("s_sel")
        s_w0 = sem("s_w0")
        s_w1_hi = sem("s_w1_hi")
        s_w1_lo = sem("s_w1_lo")
        s_x_act = sem("s_x_act")
        s_x_dve = sem("s_x_dve")
        s_xs_hi = sem("s_xs_hi")
        s_xs_lo = sem("s_xs_lo")
        s_xT_ps = sem("s_xT_ps")
        s_xT = sem("s_xT")
        s_rep_ps = sem("s_rep_ps")
        s_rep = sem("s_rep")
        s_shift = sem("s_shift")
        s_pairs = sem("s_pairs")
        s_cur0 = sem("s_cur0")
        s_cur0_hi = sem("s_cur0_hi")
        s_cur0_lo = sem("s_cur0_lo")
        s_cross0 = sem("s_cross0")
        s_y = sem("s_y")
        s_acc = sem("s_acc")
        s_scaled = sem("s_scaled")
        s_added = sem("s_added")
        s_fold = sem("s_fold")
        s_gram_ps = sem("s_gram_ps")
        s_gram = sem("s_gram")
        s_out2_ps = sem("s_out2_ps")
        s_mlp_in = sem("s_mlp_in")
        s_dT_ps = sem("s_dT_ps")
        s_h_ps = sem("s_h_ps")
        s_h = sem("s_h")

        block = ctx.enter_context(nc.Block())

        @block.sync
        def _(sp):
            def load_ids(q):
                sp.dma_start(ids_sb[:, :], ids[bass.ds(q * QUAD_B, P), :]).then_inc(s_ids, 16)

            def load_x(q):
                sp.dma_start(x_next[:, :, :],
                             scratch_chunks[:, bass.ds(q * QUAD, QUAD), :]).then_inc(s_x, 16)

            def load_diag(q, par):
                for k in range(CHUNK_B):
                    sp.dma_start(x_diag[k * D:(k + 1) * D, par, :, k * FP:(k + 1) * FP],
                                 scratch_chunks[k * D:(k + 1) * D, bass.ds(q * QUAD, QUAD), :]
                                 ).then_inc(s_diag, 16)

            def tile(q0, first, last):
                sp.wait_ge(s_permuted, q0 + TILE_QUADS)
                sp.dma_start(scratch_tiles[bass.ds(q0 * QUAD_B, P), :],
                             permuted_x[:, :, :].rearrange("p d f -> p (d f)")).then_inc(s_scratch, 16)
                if not last:
                    load_ids(q0 + TILE_QUADS)
                sp.wait_ge(s_scratch, q0 * (16 // TILE_QUADS) + 16)
                for i in range(TILE_QUADS):
                    q = q0 + i
                    if not (first and i == 0):
                        sp.wait_ge(s_x_act, q)
                        sp.wait_ge(s_x_dve, q)
                    load_x(q)
                    if not (first and i == 0):
                        sp.wait_ge(s_diag, 16 * CHUNK_B * q)
                    if not (first and i < 2):
                        sp.wait_ge(s_gram_ps, QUAD * (q - 1))
                    load_diag(q, i % 2)

            load_ids(0)
            sp.wait_ge(s_zero, 2)
            tile(0, True, False)
            with sp.Fori(TILE_QUADS, QUADS - 2 * TILE_QUADS + 1, TILE_QUADS) as q0:
                tile(q0, False, False)
            tile(QUADS - TILE_QUADS, False, True)
            sp.wait_ge(s_h, 2 * (H1 // P + H2 // P + 1))
            sp.dma_start(out.rearrange("b a -> a b"), y_sb[:, :]).then_inc(s_out, 16)
            sp.wait_ge(s_out, 16)

        @block.gpsimd
        def _(pool):
            def gather(f):
                pool.indirect_dma_start(gathered_x[:, f, :], None, tables[f],
                                        bass.IndirectOffsetOnAxis(ids_sb[:, f:f + 1].bitcast(U32), 0)
                                        ).then_inc(s_gathered, 16)

            def permute():
                pool.tensor_copy(permuted_x[:, :, 0:NF],
                                 gathered_x[:, :, :].rearrange("p f d -> p d f")).then_inc(s_permuted, TILE_QUADS)

            def add_chunk(n, par):
                for k in range(1, ACT_GROUPS):
                    w = M * GROUP_F[2 * k + 1]
                    pool.wait_ge(s_scaled, n * ACT_F + min(GF * (k + 1), ACT_F))
                    if k > 1:
                        pool.wait_ge(s_added, n * (ACT_GROUPS - 1) + k - 1)
                    pool.tensor_tensor(scaled[:, par, 0, 0:w], scaled[:, par, 0, 0:w],
                                       scaled[:, par, k, 0:w], ALU.add).then_inc(s_added, 1)

            pool.wait_ge(s_ids, 16)
            for f in range(NF):
                gather(f)
            pool.memset(permuted_x[:, :, NF:FP], 1.0).then_inc(s_zero, 1)
            pool.memset(x_diag[:, :, :, :], 0.0).then_inc(s_zero, 1)
            pool.wait_ge(s_gathered, 16 * NF)
            pool.wait_ge(s_zero, 1)
            permute()

            gather_chunks = -(-NF // GATHERS_A_CHUNK)
            with pool.Fori(0, TILES - 1) as t:
                pool.wait_ge(s_ids, 16 * (t + 2))
                for c in range(TILE_CHUNKS):
                    if c == gather_chunks:
                        pool.wait_ge(s_gathered, 16 * NF * (t + 2))
                        pool.wait_ge(s_scratch, 16 * (t + 1))
                    add_chunk(t * TILE_CHUNKS + c, c % 2)
                    if c < gather_chunks:
                        for f in range(GATHERS_A_CHUNK * c, min(GATHERS_A_CHUNK * (c + 1), NF)):
                            gather(f)
                    if c == gather_chunks:
                        permute()
            with pool.Fori(0, TILE_CHUNKS // 2) as c2:
                for par in range(2):
                    add_chunk((TILES - 1) * TILE_CHUNKS + 2 * c2 + par, par)

        @block.tensor
        def _(pe):
            def transpose_x(q, first):
                pe.wait_ge(s_xs_lo, q + 1)
                if not first:
                    pe.wait_ge(s_pairs, BLOCKS * q)
                for c in range(QUAD):
                    mm = pe.transpose(sel_ps[:, 0, c * P:(c + 1) * P], x_split[:, c, :].bitcast(F32),
                                      ident[:, :])
                mm.then_inc(s_xT_ps, 1)

            def repeat_x(q, tiles_done):
                if tiles_done is not None:
                    pe.wait_ge(s_mlp_in, 2 * tiles_done + 2)
                pe.wait_ge(s_xT, q + 1)
                pe.matmul(sel_ps[:, 1, :], sel[:, BLOCKS, :], xT[:, :], start=True, stop=True
                          ).then_inc(s_rep_ps, 1)

            def shift_x(q, j):
                if j == 1:
                    pe.wait_ge(s_rep, q + 1)
                if j >= 2:
                    pe.wait_ge(s_pairs, BLOCKS * q + j - 1)
                pe.matmul(sel_ps[:, j % 2, :], sel[:, j, :], xT[:, :], start=True, stop=True
                          ).then_inc(s_shift, 1)

            def layer0(q, j, first):
                pe.wait_ge(s_pairs, BLOCKS * q + j + 1)
                if j == 0 and not first:
                    pe.wait_ge(s_cur0_lo, 2 * q)
                pe.matmul(cur0_ps[:, :], w0_sym[:, j, :], pairs[:, j % 3, :], start=(j == 0),
                          stop=(j == BLOCKS - 1)).then_inc(s_cur0, 1)

            def gram_chunk(q, c, n, par, first):
                pe.wait_ge(s_fold, 3 * (n + 1))
                pe.wait_ge(s_diag, 16 * CHUNK_B * (q + 1))
                if not first:
                    pe.wait_ge(s_gram, n)
                pe.matmul(gram_ps[:, 0:CHUNK_B * FP], cur1[:, c % 2, :],
                          x_diag[:, bass.ds(par, 1), c, :].rearrange("p a n -> p (a n)"),
                          start=True, stop=True).then_inc(s_gram_ps, 1)

            def group(q, pos, first):
                c, j = divmod(pos, GROUPS)
                w = M * GROUP_F[j]
                if not (first and pos < Y_BANKS):
                    if pos % 2 == 0:
                        pe.wait_ge(s_acc, dve_done(q, pos - Y_BANKS))
                    else:
                        pe.wait_ge(s_scaled, act_done(q, pos - Y_BANKS))
                if pos == 0:
                    pe.wait_ge(s_cur0_lo, 2 * q + 1)
                if pos == 3 * GROUPS:
                    pe.wait_ge(s_cur0_lo, 2 * q + 2)
                y = y_ps[:, pos % Y_BANKS, 0:w]
                ws = slice(j * GF * M, j * GF * M + w)
                xs = slice(c * P, (c + 1) * P)
                pe.matmul(y, cur0_hi[:, xs], w1_hi[:, ws], start=True, stop=False)
                pe.matmul(y, cur0_hi[:, xs], w1_lo[:, ws], start=False, stop=False)
                pe.matmul(y, cur0_lo[:, xs], w1_hi[:, ws], start=False, stop=True).then_inc(s_y, 1)

            def quad(q, first=False, last=False, tiles_done=None):
                for pos in range(POSITIONS):
                    group(q, pos, first)
                    if not last:
                        if pos == PE_TRANSPOSE:
                            transpose_x(q + 1, False)
                        if pos == PE_REP:
                            repeat_x(q + 1, tiles_done)
                        if pos in PE_SHIFT:
                            shift_x(q + 1, PE_SHIFT.index(pos))
                        if pos in PE_W0:
                            layer0(q + 1, PE_W0.index(pos), False)
                    c, j = divmod(pos, GROUPS)
                    if j == PE_GRAM and not (first and c < 2):
                        behind = 1 if c < 2 else 0
                        gram_chunk(q - behind, (c - 2) % QUAD, QUAD * q + c - 2, (q - behind) % 2, first and c == 2)

            def layer2(t):
                pe.wait_ge(s_gram, TILE_CHUNKS * (t + 1))
                for f in range(NF):
                    mm = pe.matmul(sel_ps[:, 1, 0:P], w2_sb[:, f * M:(f + 1) * M],
                                   gram[:, f, bass.ds((t % 2) * P, P)], start=(f == 0), stop=(f == NF - 1))
                mm.then_inc(s_out2_ps, 1)

            pe.wait_ge(s_sel_in, 32)
            pe.wait_ge(s_dense_in, 16)
            for t in range(TILES):
                mm = pe.transpose(y_ps[:, t // 4, (t % 4) * P:(t % 4 + 1) * P], dense_sb[:, t, :], ident[:, :])
            mm.then_inc(s_dT_ps, 1)
            pe.wait_ge(s_sel, 1)
            transpose_x(0, True)
            repeat_x(0, None)
            pe.wait_ge(s_w0, 1)
            shift_x(0, 0)
            shift_x(0, 1)
            for j in range(BLOCKS):
                layer0(0, j, True)
                if j + 2 < BLOCKS:
                    shift_x(0, j + 2)
            pe.wait_ge(s_w1_lo, 1)
            pe.wait_ge(s_mlp_in, 2)

            quad(0, first=True)
            pe.wait_ge(s_rest_in, 16 * 7)
            with pe.Fori(0, TILES - 1) as t:
                with pe.Fori(0, TILE_QUADS) as i:
                    quad(t * TILE_QUADS + i + 1, tiles_done=t)
                layer2(t)
            with pe.Fori(QUADS - TILE_QUADS + 1, QUADS - 1) as q:
                quad(q, tiles_done=TILES - 1)
            quad(QUADS - 1, last=True)
            for c in (QUAD - 2, QUAD - 1):
                gram_chunk(QUADS - 1, c, CHUNKS - QUAD + c, (QUADS - 1) % 2, False)
            layer2(TILES - 1)

            done = 0
            for half in range(2):
                cols = slice(half * 512, half * 512 + 512)
                pe.wait_ge(s_mlp_in, 2 * TILES + 2)
                for mb in range(H1 // P):
                    if half:
                        pe.wait_ge(s_h, mb + 1)
                    for k, src in enumerate((cross0T, cross1T, denseT, cross2T)):
                        row = (0, 1, 3, 2)[k]
                        mm = pe.matmul(y_ps[:, mb, :], wt1[:, row, mb * P:(mb + 1) * P], src[:, cols],
                                       start=(k == 0), stop=(k == 3))
                    mm.then_inc(s_h_ps, 1)
                done += H1 // P
                for nb in range(H2 // P):
                    pe.wait_ge(s_h, done)
                    for k in range(H1 // P):
                        mm = pe.matmul(sel_ps[:, nb, :], wt2[:, k, nb * P:(nb + 1) * P], h1T[:, k, :],
                                       start=(k == 0), stop=(k == H1 // P - 1))
                    mm.then_inc(s_h_ps, 1)
                done += H2 // P
                pe.wait_ge(s_h, done)
                for k in range(H2 // P):
                    mm = pe.matmul(cur0_ps[0:1, :], wt3[:, k:k + 1], h2T[:, k, :],
                                   start=(k == 0), stop=(k == H2 // P - 1))
                mm.then_inc(s_h_ps, 1)
                done += 1

        @block.scalar
        def _(act):
            def split_x_hi(q):
                act.wait_ge(s_x, 16 * (q + 1))
                act.activation(x_split[:, :, 0:FP], x_next[:, :, :], ACT.Copy).then_inc(s_xs_hi, 1)

            def copy_xT(q):
                act.wait_ge(s_xT_ps, q + 1)
                act.activation(xT[:, :], sel_ps[:, 0, :], ACT.Copy).then_inc(s_xT, 1)

            def copy_rep(q):
                act.wait_ge(s_rep_ps, q + 1)
                act.activation(rep[:, :], sel_ps[:, 1, :], ACT.Copy).then_inc(s_rep, 1)

            def cur0_hi_part(q, hi):
                cols = slice(LO, COLS) if hi else slice(0, LO)
                if hi:
                    act.wait_ge(s_cross0, q + 1)
                else:
                    act.wait_ge(s_cur0, BLOCKS * (q + 1))
                act.activation(cur0_hi[:, cols], cur0_ps[:, cols], ACT.Copy).then_inc(s_cur0_hi, 1)

            def copy_gram(n):
                act.wait_ge(s_gram_ps, n + 1)
                at = (n * CHUNK_B) % (2 * P)
                act.activation(gram[:, :, bass.ds(at, CHUNK_B)].rearrange("p f b -> p b f"),
                               gram_ps[:, 0:CHUNK_B * FP].rearrange("p (b f) -> p b f", f=FP),
                               ACT.Copy).then_inc(s_gram, 1)

            def group(q, pos, first):
                c, j = divmod(pos, GROUPS)
                n = QUAD * q + c
                act.wait_ge(s_y, POSITIONS * q + pos + 1)
                if j == 1 and not (first and c < 2):
                    act.wait_ge(s_fold, 3 * (n - 2) + 1)
                for k in range(GROUP_F[j]):
                    f = GF * j + k
                    act.activation(scaled[:, c % 2, j // 2, k * M:(k + 1) * M],
                                   y_ps[:, pos % Y_BANKS, k * M:(k + 1) * M], ACT.Copy,
                                   scale=x_act[:, c, f:f + 1]).then_inc(s_scaled, 1)

            def quad(q, first=False, last=False):
                if not first:
                    act.wait_ge(s_scaled, QUAD * ACT_F * q)
                act.wait_ge(s_x, 16 * (q + 1))
                act.activation(x_act[:, :, :], x_next[:, :, :], ACT.Copy).then_inc(s_x_act, 1)
                act.wait_ge(s_x_act, q + 1)
                for pos in range(1, POSITIONS, 2):
                    group(q, pos, first)
                    if pos == ACT_CUR0_HI:
                        cur0_hi_part(q, True)
                    if not last:
                        if pos == ACT_XSPLIT:
                            split_x_hi(q + 1)
                        if pos == ACT_XT:
                            copy_xT(q + 1)
                        if pos == ACT_REP:
                            copy_rep(q + 1)
                        if pos == ACT_CUR0_LO:
                            cur0_hi_part(q + 1, False)
                    c, j = divmod(pos, GROUPS)
                    if j == ACT_GRAM and not (first and c < 2):
                        copy_gram(QUAD * q + c - 2)

            def cross12(t):
                act.wait_ge(s_out2_ps, t + 1)
                act.activation(cross1T[:, bass.ds(t * P, P)], gram[:, NF, bass.ds((t % 2) * P, P)],
                               ACT.Copy).then_inc(s_mlp_in, 1)
                act.activation(cross2T[:, bass.ds(t * P, P)], sel_ps[:, 1, 0:P],
                               ACT.Copy).then_inc(s_mlp_in, 1)

            act.dma_start(sel_stage, selectors.rearrange("j p r -> p j r")).then_inc(s_sel_in, 16)
            act.dma_start(ident[:, :], identity).then_inc(s_sel_in, 16)
            act.dma_start(pair_stage, w0_pair.rearrange("j p m -> p j m")).then_inc(s_w0_in, 16)
            act.dma_start(twin_stage, w0_twin.rearrange("j p m -> p j m")).then_inc(s_w0_in, 16)
            act.dma_start(f1_stage.rearrange("g (f m) -> g f m", m=M),
                          f1.rearrange("(f g) m -> g f m", g=M)).then_inc(s_f1_in, 16)
            act.wait_ge(s_zeroD, 3)
            act.dma_start(dense_sb[:, :, 0:DENSE], dense.rearrange("(t p) k -> p t k", p=P)).then_inc(s_dense_in, 16)
            act.dma_start(wt1[:, 0:3, :], w_top1[0:3 * M, :].rearrange("(k p) n -> p k n", p=P)).then_inc(s_rest_in, 16)
            act.dma_start(wt1[0:DENSE, 3, :], w_top1[3 * M:3 * M + DENSE, :]).then_inc(s_rest_in, 16)
            act.dma_start(w2_sb[:, :].rearrange("g (f m) -> g f m", m=M),
                          f2.rearrange("(f g) m -> g f m", g=M)).then_inc(s_rest_in, 16)
            act.dma_start(wt2[:, :, :], w_top2.rearrange("(k p) n -> p k n", p=P)).then_inc(s_rest_in, 16)
            act.dma_start(wt3[:, :], w_top3.rearrange("(k p) a -> p (k a)", p=P),
                          allow_slow_non_contiguous=True).then_inc(s_rest_in, 16)
            act.dma_start(bt1[:, :], b_top1.rearrange("(k p) -> p k", p=P),
                          allow_slow_non_contiguous=True).then_inc(s_rest_in, 16)
            act.dma_start(bt2[:, :], b_top2.rearrange("(k p) -> p k", p=P),
                          allow_slow_non_contiguous=True).then_inc(s_rest_in, 16)

            act.wait_ge(s_sel_in, 32)
            act.activation(sel[:, :, :], sel_stage, ACT.Copy).then_inc(s_sel, 1)
            act.wait_ge(s_f1_in, 16)
            act.activation(w1_hi[:, :], f1_stage, ACT.Copy).then_inc(s_w1_hi, 1)
            act.wait_ge(s_dT_ps, 1)
            for i in range(2):
                act.activation(denseT[:, i * 512:(i + 1) * 512], y_ps[:, i, :], ACT.Copy).then_inc(s_mlp_in, 1)

            split_x_hi(0)
            copy_xT(0)
            copy_rep(0)
            cur0_hi_part(0, False)
            quad(0, first=True)
            with act.Fori(0, TILES - 1) as t:
                with act.Fori(0, TILE_QUADS) as i:
                    quad(t * TILE_QUADS + i + 1)
                cross12(t)
            with act.Fori(QUADS - TILE_QUADS + 1, QUADS - 1) as q:
                quad(q)
            quad(QUADS - 1, last=True)
            copy_gram(CHUNKS - 2)
            copy_gram(CHUNKS - 1)
            cross12(TILES - 1)

            act.wait_ge(s_rest_in, 16 * 7)
            done = 0
            for half in range(2):
                for mb in range(H1 // P):
                    done += 1
                    act.wait_ge(s_h_ps, done)
                    act.activation(h1T[:, mb, :], y_ps[:, mb, :], ACT.Relu, bias=bt1[:, mb:mb + 1]).then_inc(s_h, 1)
                for nb in range(H2 // P):
                    done += 1
                    act.wait_ge(s_h_ps, done)
                    act.activation(h2T[:, nb, :], sel_ps[:, nb, :], ACT.Relu, bias=bt2[:, nb:nb + 1]).then_inc(s_h, 1)
                done += 1
                act.wait_ge(s_h_ps, done)
                act.activation(y_sb[:, half * 512:(half + 1) * 512], cur0_ps[0:1, :], ACT.Copy).then_inc(s_h, 1)

        @block.vector
        def _(dve):
            def split_x_lo(q):
                dve.wait_ge(s_xs_hi, q + 1)
                dve.tensor_tensor(x_split[:, :, FP:2 * FP], x_next[:, :, :],
                                  x_split[:, :, 0:FP].bitcast(F32), ALU.subtract).then_inc(s_xs_lo, 1)

            def make_pairs(q, j, first):
                dve.wait_ge(s_shift, BLOCKS * q + j + 1)
                if j == 0:
                    dve.wait_ge(s_rep, q + 1)
                if j >= 3:
                    dve.wait_ge(s_cur0, BLOCKS * q + j - 2)
                elif not first:
                    dve.wait_ge(s_cur0, BLOCKS * q)
                dve.tensor_tensor(pairs[:, j % 3, :], sel_ps[:, j % 2, :], rep[:, :], ALU.mult).then_inc(s_pairs, 1)

            def cur0_lo_part(q, hi):
                cols = slice(LO, COLS) if hi else slice(0, LO)
                dve.wait_ge(s_cur0_hi, 2 * q + (2 if hi else 1))
                dve.tensor_tensor(cur0_lo[:, cols], cur0_ps[:, cols], cur0_hi[:, cols].bitcast(F32),
                                  ALU.subtract).then_inc(s_cur0_lo, 1)

            def sum_cross0(q):
                dve.tensor_reduce(cross0T[:, bass.ds(q * QUAD_B, QUAD_B)],
                                  cur0_ps[:, :].rearrange("p (b d) -> p b d", d=D), AX.X, ALU.add).then_inc(s_cross0, 1)

            def group(q, pos, first):
                c, j = divmod(pos, GROUPS)
                if j == 0 and not (first and c < 2):
                    dve.wait_ge(s_fold, 3 * (QUAD * q + c - 2) + 2)
                dve.wait_ge(s_y, POSITIONS * q + pos + 1)
                for k in range(GF):
                    f = GF * j + k
                    y = y_ps[:, pos % Y_BANKS, k * M:(k + 1) * M]
                    a = acc[:, c % 2, (k % 2) * M:(k % 2 + 1) * M]
                    x = x_dve[:, c, f:f + 1]
                    if j == 0 and k < 2:
                        dve.tensor_scalar(a, y, x, None, ALU.mult).then_inc(s_acc, 1)
                    else:
                        dve.wait_ge(s_acc, q * (QUAD * DVE_F) + c * DVE_F + GF * (j // 2) + k - 1)
                        dve.scalar_tensor_tensor(out=a, in0=y, scalar=x, in1=a, op0=ALU.mult,
                                                 op1=ALU.add).then_inc(s_acc, 1)

            def fold_chunk(n, par, step, first):
                if step == 0:
                    dve.wait_ge(s_added, (ACT_GROUPS - 1) * (n + 1))
                    dve.tensor_tensor(fold[:, 0, :], scaled[:, par, 0, 0:2 * M], scaled[:, par, 0, 2 * M:4 * M],
                                      ALU.add).then_inc(s_fold, 1)
                if step == 1:
                    dve.wait_ge(s_fold, 3 * n + 1)
                    dve.tensor_tensor(fold[:, 1, :], fold[:, 0, :], acc[:, par, :], ALU.add).then_inc(s_fold, 1)
                if step == 2:
                    if not first:
                        dve.wait_ge(s_gram_ps, n - 1)
                    dve.wait_ge(s_fold, 3 * n + 2)
                    dve.tensor_tensor(cur1[:, par, :], fold[:, 1, 0:M], fold[:, 1, M:2 * M], ALU.add).then_inc(s_fold, 1)

            def quad(q, first=False, last=False):
                if not first:
                    dve.wait_ge(s_acc, QUAD * DVE_F * q)
                dve.wait_ge(s_x, 16 * (q + 1))
                dve.tensor_copy(x_dve[:, :, :], x_next[:, :, :]).then_inc(s_x_dve, 1)
                dve.wait_ge(s_x_dve, q + 1)
                for pos in range(0, POSITIONS, 2):
                    group(q, pos, first)
                    if pos == DVE_CUR0_HI:
                        cur0_lo_part(q, True)
                    if not last:
                        if pos == DVE_XSPLIT:
                            split_x_lo(q + 1)
                        if pos in DVE_PAIRS:
                            make_pairs(q + 1, DVE_PAIRS.index(pos), False)
                        if pos == DVE_CUR0_LO:
                            cur0_lo_part(q + 1, False)
                        if pos == DVE_CROSS0:
                            sum_cross0(q + 1)
                    c, j = divmod(pos, GROUPS)
                    if j in DVE_FOLD and not (first and c == 0):
                        fold_chunk(QUAD * q + c - 1, (c - 1) % 2, DVE_FOLD.index(j), first and c < 3)

            dve.memset(dense_sb[:, :, :], 0.0).then_inc(s_zeroD, 1)
            dve.memset(wt1[:, 3, :], 0.0).then_inc(s_zeroD, 1)
            dve.memset(x_split[:, :, :].bitcast(F32), 0.0).then_inc(s_zeroD, 1)
            dve.wait_ge(s_w0_in, 32)
            dve.tensor_tensor(w0_sym[:, :, :], pair_stage, twin_stage, ALU.add).then_inc(s_w0, 1)
            dve.wait_ge(s_w1_hi, 1)
            dve.tensor_tensor(w1_lo[:, :], f1_stage, w1_hi[:, :].bitcast(F32), ALU.subtract).then_inc(s_w1_lo, 1)

            split_x_lo(0)
            for j in range(BLOCKS):
                make_pairs(0, j, True)
            cur0_lo_part(0, False)
            sum_cross0(0)
            quad(0, first=True)
            with dve.Fori(1, QUADS - 1) as q:
                quad(q)
            quad(QUADS - 1, last=True)
            for step in range(3):
                fold_chunk(CHUNKS - 1, (CHUNKS - 1) % 2, step, False)


def kernel(**inputs):
    import concourse.bacc as bacc
    from concourse.bass_utils import run_bass_kernel_spmd

    nc = bacc.Bacc("TRN2", target_bir_lowering=False, num_devices=1)
    arrays = {}

    def arg(name, a):
        a = np.ascontiguousarray(a)
        arrays[f"in_{name}"] = a
        return nc.dram_tensor(f"in_{name}", a.shape, mybir.dt.from_np(a.dtype), kind="ExternalInput").ap()

    f0 = np.asarray(inputs["L0_rec_f0"]).reshape(NF, NF, M)
    w0_pair = np.zeros((BLOCKS, P, M), f0.dtype)
    w0_twin = np.zeros((BLOCKS, P, M), f0.dtype)
    selectors = np.zeros((BLOCKS + 1, P, P), np.float32)
    for s in range(SHIFTS):
        j, r = divmod(s, BLOCK_SHIFTS)
        for f in range(NF):
            g = (f + s) % NF
            row = r * NF + f
            w0_pair[j, row] = f0[f, g]
            if s:
                w0_twin[j, row] = f0[g, f]
            selectors[j, [g, FP + g], row] = 1.0
            selectors[BLOCKS, [f, FP + f], row] = 1.0

    args = dict(
        dense=arg("dense", inputs["dense_ctx"]),
        ids=arg("ids", inputs["ids"]),
        tables=[arg(f"tbl_{f}", inputs[f"tbl_{f}"]) for f in range(NF)],
        w_top1=arg("w_top1", inputs["W_top1"]),
        b_top1=arg("b_top1", inputs["b_top1"]),
        w_top2=arg("w_top2", inputs["W_top2"]),
        b_top2=arg("b_top2", inputs["b_top2"]),
        w_top3=arg("w_top3", inputs["W_top3"]),
        w0_pair=arg("w0_pair", w0_pair),
        w0_twin=arg("w0_twin", w0_twin),
        f1=arg("f1", inputs["L0_rec_f1"]),
        f2=arg("f2", inputs["L0_rec_f2"]),
        selectors=arg("selectors", selectors),
        identity=arg("identity", np.eye(P, dtype=np.float32)),
    )
    out = nc.dram_tensor("out_y", (BATCH, 1), F32, kind="ExternalOutput").ap()
    build(nc, out=out, **args)
    r = run_bass_kernel_spmd(nc, [arrays], core_ids=[0])
    return r.results[0]["out_y"]
```

```python
from contextlib import ExitStack

import numpy as np

import concourse.bass as bass
from concourse import mybir

F32 = mybir.dt.float32
F32R = mybir.dt.float32r
I32 = mybir.dt.int32
U32 = mybir.dt.uint32
ALU = mybir.AluOpType
ACT = mybir.ActivationFunctionType
AX = mybir.AxisListType

BATCH = 1024
NF = 39
D = 16
M = 128
DENSE = 16
H1, H2 = 512, 256

P = 128
FP = NF + 1
CHUNK_B = P // D
QUAD = 4
COLS = QUAD * P
QUAD_B = QUAD * CHUNK_B
QUADS = BATCH // QUAD_B
TILES = BATCH // P
TILE_QUADS = QUADS // TILES
TILE_CHUNKS = TILE_QUADS * QUAD
CHUNKS = QUADS * QUAD

SHIFTS = (NF + 1) // 2
BLOCK_SHIFTS = 3
BLOCKS = -(-SHIFTS // BLOCK_SHIFTS)

GF = 4
GROUPS = -(-NF // GF)
GROUP_F = [min(GF, NF - GF * j) for j in range(GROUPS)]
POSITIONS = QUAD * GROUPS
DVE_GROUPS = [0, 2, 4, 6, 8]
ACT_GROUPS = [j for j in range(GROUPS) if j not in DVE_GROUPS]
DVE_F = sum(GROUP_F[j] for j in DVE_GROUPS)
ACT_F = sum(GROUP_F[j] for j in ACT_GROUPS)
ADDS = len(ACT_GROUPS) - 1
Y_BANKS = 5
assert GROUPS % Y_BANKS == 0 and GROUP_F[ACT_GROUPS[0]] == GF

PE_W0 = [6, 9, 16, 21, 24, 28, 31]
DVE_PAIRS = [0, 4, 10, 14, 16, 22, 28]
ACT_CUR0_LO, ACT_CUR0_HI = 31, 1
DVE_CUR0_LO, DVE_CROSS0, DVE_CUR0_HI = 30, 38, 0
PE_GRAM = 5
ACT_GRAM = 9
DVE_FOLD = [4, 6, 8]
LO = 3 * P
SLOTS = 3
FIRST_HALF = 4
GATHERED_AT = 9


def taken(groups, pos):
    c, last = divmod(pos, GROUPS)
    return c * sum(GROUP_F[j] for j in groups) + sum(GROUP_F[j] for j in groups if j <= last)


def build(nc, dense, ids, tables, w_top1, b_top1, w_top2, b_top2, w_top3, w0_pair, w0_twin, f1, f2,
          identity, out):
    scratch = nc.dram_tensor("x0_by_column", [BATCH * D, FP], F32, kind="Internal").ap()
    scratch_tiles = scratch.rearrange("(b d) f -> b (d f)", d=D)
    scratch_chunks = scratch.rearrange("(n p) f -> p n f", p=P)

    rows = NF + BLOCKS * BLOCK_SHIFTS - 1
    scratchT = nc.dram_tensor("x0_by_feature", [rows, BATCH * D], F32, kind="Internal").ap()
    scratchT_samples = scratchT.rearrange("f (b d) -> b f d", d=D)

    with ExitStack() as ctx:
        def sb(name, shape, dt=F32):
            return ctx.enter_context(nc.sbuf_tensor(name, shape, dt))

        def psum(name, shape):
            return ctx.enter_context(nc.psum_tensor(name, shape, F32))

        def sem(name):
            return ctx.enter_context(nc.semaphore(name))

        w1_hi = sb("w1_hi", [P, NF * M], F32R)
        w1_lo = sb("w1_lo", [P, NF * M], F32R)
        w2_sb = sb("w2_sb", [P, NF * M])
        w0_sym = sb("w0_sym", [P, BLOCKS, M])
        ident = sb("ident", [P, P])
        wt1 = sb("wt1", [P, 4, H1])
        wt2 = sb("wt2", [P, H1 // P, H2])
        wt3 = sb("wt3", [P, H2 // P])
        bt1 = sb("bt1", [P, H1 // P])
        bt2 = sb("bt2", [P, H2 // P])
        ids_sb = sb("ids_sb", [P, NF], I32)
        gathered_x = sb("gathered_x", [P, NF, D])
        permuted_x = sb("permuted_x", [P, D, FP])
        x_next = sb("x_next", [P, QUAD, FP])
        x_dve = sb("x_dve", [P, QUAD, FP])
        x_act = sb("x_act", [P, QUAD, FP])
        x_diag = sb("x_diag", [P, 2, QUAD, CHUNK_B * FP])
        x_rep = sb("x_rep", [P, COLS])
        x_shift = sb("x_shift", [P, BLOCKS, COLS])
        pairs = sb("pairs", [P, SLOTS, COLS])
        cur0_hi = sb("cur0_hi", [P, COLS], F32R)
        cur0_lo = sb("cur0_lo", [P, COLS], F32R)
        scaled = sb("scaled", [P, 2, len(ACT_GROUPS), GF * M])
        acc = sb("acc", [P, 2, 2 * M])
        fold = sb("fold", [P, 2, 2 * M])
        cur1 = sb("cur1", [P, 2, M])
        gram = sb("gram", [P, FP, 2 * P])
        cross0T = sb("cross0T", [P, BATCH])
        cross1T = sb("cross1T", [P, BATCH])
        cross2T = sb("cross2T", [P, BATCH])
        denseT = sb("denseT", [P, BATCH])
        y_sb = sb("y_sb", [1, BATCH])

        stage = gram[:, :, :].rearrange("p f b -> p (f b)")
        f1_stage = stage[:, 0:NF * M]
        o = NF * M
        pair_stage = stage[:, o:o + BLOCKS * M].rearrange("p (j m) -> p j m", m=M)
        o += BLOCKS * M
        twin_stage = stage[:, o:o + BLOCKS * M].rearrange("p (j m) -> p j m", m=M)
        dense_sb = scaled[:, 0, 0:2, :].rearrange("p a (t k) -> p (a t) k", k=P)
        h1T = scaled[:, 0, 0:H1 // P, :]
        h2T = scaled[:, 1, 0:H2 // P, :]

        y_ps = psum("y_ps", [P, Y_BANKS, 512])
        out2_ps = psum("out2_ps", [P, 512])
        cur0_ps = psum("cur0_ps", [P, 512])
        gram_ps = psum("gram_ps", [P, 512])

        h2_ps = [y_ps[:, 4, :], out2_ps[:, :]]

        s_ids = sem("s_ids")
        s_gathered = sem("s_gathered")
        s_permuted = sem("s_permuted")
        s_scratch = sem("s_scratch")
        s_scratchT = sem("s_scratchT")
        s_x = sem("s_x")
        s_shift0 = sem("s_shift0")
        s_shift1 = sem("s_shift1")
        s_diag = sem("s_diag")
        s_ident_in = sem("s_ident_in")
        s_w0_in = sem("s_w0_in")
        s_f1_in = sem("s_f1_in")
        s_rest_in = sem("s_rest_in")
        s_dense_in = sem("s_dense_in")
        s_out = sem("s_out")
        s_zero = sem("s_zero")
        s_zeroD = sem("s_zeroD")
        s_w0 = sem("s_w0")
        s_w1_hi = sem("s_w1_hi")
        s_w1_lo = sem("s_w1_lo")
        s_x_act = sem("s_x_act")
        s_x_dve = sem("s_x_dve")
        s_pairs = sem("s_pairs")
        s_cur0 = sem("s_cur0")
        s_cur0_hi = sem("s_cur0_hi")
        s_cur0_lo = sem("s_cur0_lo")
        s_cross0 = sem("s_cross0")
        s_y = sem("s_y")
        s_acc = sem("s_acc")
        s_scaled = sem("s_scaled")
        s_added = sem("s_added")
        s_fold = sem("s_fold")
        s_gram_ps = sem("s_gram_ps")
        s_gram = sem("s_gram")
        s_out2_ps = sem("s_out2_ps")
        s_mlp_in = sem("s_mlp_in")
        s_dT_ps = sem("s_dT_ps")
        s_h_ps = sem("s_h_ps")
        s_h = sem("s_h")

        block = ctx.enter_context(nc.Block())

        @block.sync
        def _(sp):
            def load_ids(q):
                sp.dma_start(ids_sb[:, :], ids[bass.ds(q * QUAD_B, P), :]).then_inc(s_ids, 16)

            def load_x(q):
                sp.dma_start(x_next[:, :, :],
                             scratch_chunks[:, bass.ds(q * QUAD, QUAD), :]).then_inc(s_x, 16)

            def load_diag(q, par):
                for k in range(CHUNK_B):
                    sp.dma_start(x_diag[k * D:(k + 1) * D, par, :, k * FP:(k + 1) * FP],
                                 scratch_chunks[k * D:(k + 1) * D, bass.ds(q * QUAD, QUAD), :]
                                 ).then_inc(s_diag, 16)

            def load_shift(q, half):
                j0, j1 = (0, FIRST_HALF) if half == 0 else (FIRST_HALF, BLOCKS)
                for s in range(BLOCK_SHIFTS):
                    at = slice(s * NF, (s + 1) * NF)
                    source = bass.AP(tensor=scratchT.tensor, offset=(s + j0 * BLOCK_SHIFTS) * BATCH * D + q * COLS,
                                     ap=[[BATCH * D, NF], [BLOCK_SHIFTS * BATCH * D, j1 - j0], [1, COLS]])
                    sp.dma_start(x_shift[at, j0:j1, :], source).then_inc(s_shift1 if half else s_shift0, 16)
                    if half:
                        sp.dma_start(x_rep[at, :], scratchT[0:NF, bass.ds(q * COLS, COLS)]).then_inc(s_shift1, 16)

            def load_pair_factors(q, first):
                if not first:
                    sp.wait_ge(s_pairs, BLOCKS * (q - 1) + FIRST_HALF)
                load_shift(q, 0)
                if not first:
                    sp.wait_ge(s_pairs, BLOCKS * q)
                load_shift(q, 1)

            def load_quad(q, half, first, second):
                if not first:
                    sp.wait_ge(s_diag, 16 * CHUNK_B * q)
                    sp.wait_ge(s_x_act, q)
                    sp.wait_ge(s_x_dve, q)
                load_x(q)
                if not (first or second):
                    sp.wait_ge(s_gram_ps, QUAD * (q - 1))
                load_diag(q, half)

            def write_tile(q0):
                sp.wait_ge(s_permuted, q0 + TILE_QUADS)
                tile_rows = bass.ds(q0 * QUAD_B, P)
                sp.dma_start(scratchT_samples[tile_rows, 0:NF, :], gathered_x[:, :, :]).then_inc(s_scratchT, 16)
                sp.dma_start(scratchT_samples[tile_rows, NF:rows, :],
                             gathered_x[:, 0:rows - NF, :]).then_inc(s_scratchT, 16)
                sp.dma_start(scratch_tiles[tile_rows, :],
                             permuted_x[:, :, :].rearrange("p d f -> p (d f)")).then_inc(s_scratch, 16)

            def tile(q0, first, last):
                for i in range(TILE_QUADS):
                    q = q0 + i
                    if i == 0:
                        write_tile(q0)
                        if not last:
                            load_ids(q0 + TILE_QUADS)
                        sp.wait_ge(s_scratchT, q0 * (32 // TILE_QUADS) + 32)
                        sp.wait_ge(s_scratch, q0 * (16 // TILE_QUADS) + 16)
                    load_pair_factors(q, first and i == 0)
                    load_quad(q, i % 2, first and i == 0, first and i == 1)

            load_ids(0)
            sp.wait_ge(s_zero, 2)
            sp.wait_ge(s_zeroD, 4)
            tile(0, True, False)
            with sp.Fori(TILE_QUADS, QUADS - 2 * TILE_QUADS + 1, TILE_QUADS) as q0:
                tile(q0, False, False)
            tile(QUADS - TILE_QUADS, False, True)
            sp.wait_ge(s_h, 2 * (H1 // P + H2 // P + 1))
            sp.dma_start(out.rearrange("b a -> a b"), y_sb[:, :]).then_inc(s_out, 16)
            sp.wait_ge(s_out, 16)

        @block.gpsimd
        def _(pool):
            def gather(f):
                pool.indirect_dma_start(gathered_x[:, f, :], None, tables[f],
                                        bass.IndirectOffsetOnAxis(ids_sb[:, f:f + 1].bitcast(U32), 0)
                                        ).then_inc(s_gathered, 16)

            def permute():
                pool.tensor_copy(permuted_x[:, :, 0:NF],
                                 gathered_x[:, :, :].rearrange("p f d -> p d f")).then_inc(s_permuted, TILE_QUADS)

            def add_chunk(n, par):
                for k in range(1, len(ACT_GROUPS)):
                    w = M * GROUP_F[ACT_GROUPS[k]]
                    pool.wait_ge(s_scaled, n * ACT_F + taken(ACT_GROUPS, ACT_GROUPS[k]))
                    if k > 1:
                        pool.wait_ge(s_added, n * ADDS + k - 1)
                    pool.tensor_tensor(scaled[:, par, 0, 0:w], scaled[:, par, 0, 0:w],
                                       scaled[:, par, k, 0:w], ALU.add).then_inc(s_added, 1)

            def start_gathers(t):
                pool.wait_ge(s_ids, 16 * (t + 1))
                pool.wait_ge(s_scratchT, 32 * t)

            share = [NF * i // TILE_CHUNKS for i in range(TILE_CHUNKS + 1)]
            early = TILE_CHUNKS - GATHERED_AT

            def tile(t, more):
                for c in range(TILE_CHUNKS):
                    if c == GATHERED_AT:
                        pool.wait_ge(s_gathered, 16 * NF * (t + 2))
                        pool.wait_ge(s_scratch, 16 * (t + 1))
                    if c == GATHERED_AT + 1 and more:
                        start_gathers(t + 2)
                    add_chunk(t * TILE_CHUNKS + c, c % 2)
                    if c < GATHERED_AT:
                        i = c + early
                        for f in range(share[i], share[i + 1]):
                            gather(f)
                    if c == GATHERED_AT:
                        permute()
                    if c > GATHERED_AT and more:
                        i = c - GATHERED_AT
                        for f in range(share[i - 1] if i > 1 else 0, share[i] if c < TILE_CHUNKS - 1 else share[early]):
                            gather(f)

            pool.wait_ge(s_ids, 16)
            for f in range(NF):
                gather(f)
            pool.memset(permuted_x[:, :, NF:FP], 1.0).then_inc(s_zero, 1)
            pool.memset(x_diag[:, :, :, :], 0.0).then_inc(s_zero, 1)
            pool.wait_ge(s_gathered, 16 * NF)
            pool.wait_ge(s_zero, 1)
            permute()
            start_gathers(1)
            for f in range(share[early]):
                gather(f)
            with pool.Fori(0, TILES - 2) as t:
                tile(t, True)
            tile(TILES - 2, False)
            with pool.Fori(0, TILE_CHUNKS // 2) as c2:
                for par in range(2):
                    add_chunk((TILES - 1) * TILE_CHUNKS + 2 * c2 + par, par)

        @block.tensor
        def _(pe):
            def layer0(q, j, first):
                pe.wait_ge(s_pairs, BLOCKS * q + j + 1)
                if j == 0 and not first:
                    pe.wait_ge(s_cur0_lo, 2 * q)
                pe.matmul(cur0_ps[:, :], w0_sym[:, j, :], pairs[:, j % SLOTS, :], start=(j == 0),
                          stop=(j == BLOCKS - 1)).then_inc(s_cur0, 1)

            def gram_chunk(q, c, n, par, first):
                pe.wait_ge(s_fold, 3 * (n + 1))
                pe.wait_ge(s_diag, 16 * CHUNK_B * (q + 1))
                if not first:
                    pe.wait_ge(s_gram, n)
                pe.matmul(gram_ps[:, 0:CHUNK_B * FP], cur1[:, c % 2, :],
                          x_diag[:, bass.ds(par, 1), c, :].rearrange("p a n -> p (a n)"),
                          start=True, stop=True).then_inc(s_gram_ps, 1)

            def group(q, pos, first):
                c, j = divmod(pos, GROUPS)
                w = M * GROUP_F[j]
                if not (first and pos < Y_BANKS):
                    before = pos - Y_BANKS
                    if before % GROUPS in DVE_GROUPS:
                        pe.wait_ge(s_acc, q * (QUAD * DVE_F) + taken(DVE_GROUPS, before))
                    else:
                        pe.wait_ge(s_scaled, q * (QUAD * ACT_F) + taken(ACT_GROUPS, before))
                if pos == 0:
                    pe.wait_ge(s_cur0_lo, 2 * q + 1)
                if pos == 3 * GROUPS:
                    pe.wait_ge(s_cur0_lo, 2 * q + 2)
                y = y_ps[:, pos % Y_BANKS, 0:w]
                ws = slice(j * GF * M, j * GF * M + w)
                xs = slice(c * P, (c + 1) * P)
                pe.matmul(y, cur0_hi[:, xs], w1_hi[:, ws], start=True, stop=False)
                pe.matmul(y, cur0_hi[:, xs], w1_lo[:, ws], start=False, stop=False)
                pe.matmul(y, cur0_lo[:, xs], w1_hi[:, ws], start=False, stop=True).then_inc(s_y, 1)

            def quad(q, first=False, last=False):
                for pos in range(POSITIONS):
                    group(q, pos, first)
                    if not last:
                        if pos in PE_W0:
                            layer0(q + 1, PE_W0.index(pos), False)
                    c, j = divmod(pos, GROUPS)
                    if j == PE_GRAM and not (first and c < 2):
                        behind = 1 if c < 2 else 0
                        gram_chunk(q - behind, (c - 2) % QUAD, QUAD * q + c - 2, (q - behind) % 2, first and c == 2)

            def layer2(t):
                pe.wait_ge(s_gram, TILE_CHUNKS * (t + 1))
                pe.wait_ge(s_mlp_in, 2 * t + 2)
                for f in range(NF):
                    mm = pe.matmul(out2_ps[:, 0:P], w2_sb[:, f * M:(f + 1) * M],
                                   gram[:, f, bass.ds((t % 2) * P, P)], start=(f == 0), stop=(f == NF - 1))
                mm.then_inc(s_out2_ps, 1)

            pe.wait_ge(s_ident_in, 16)
            pe.wait_ge(s_dense_in, 16)
            for t in range(TILES):
                mm = pe.transpose(y_ps[:, t // 4, (t % 4) * P:(t % 4 + 1) * P], dense_sb[:, t, :], ident[:, :])
            mm.then_inc(s_dT_ps, 1)
            pe.wait_ge(s_w0, 1)
            for j in range(BLOCKS):
                layer0(0, j, True)
            pe.wait_ge(s_w1_lo, 1)
            pe.wait_ge(s_mlp_in, 2)

            quad(0, first=True)
            pe.wait_ge(s_rest_in, 16 * 7)
            with pe.Fori(0, TILES - 1) as t:
                with pe.Fori(0, TILE_QUADS) as i:
                    quad(t * TILE_QUADS + i + 1)
                layer2(t)
            with pe.Fori(QUADS - TILE_QUADS + 1, QUADS - 1) as q:
                quad(q)
            quad(QUADS - 1, last=True)
            for c in (QUAD - 2, QUAD - 1):
                gram_chunk(QUADS - 1, c, CHUNKS - QUAD + c, (QUADS - 1) % 2, False)
            layer2(TILES - 1)

            done = 0
            for half in range(2):
                cols = slice(half * 512, half * 512 + 512)
                pe.wait_ge(s_mlp_in, 2 * TILES + 2)
                for mb in range(H1 // P):
                    if half:
                        pe.wait_ge(s_h, mb + 1)
                    for k, src in enumerate((cross0T, cross1T, denseT, cross2T)):
                        row = (0, 1, 3, 2)[k]
                        mm = pe.matmul(y_ps[:, mb, :], wt1[:, row, mb * P:(mb + 1) * P], src[:, cols],
                                       start=(k == 0), stop=(k == 3))
                    mm.then_inc(s_h_ps, 1)
                done += H1 // P
                for nb in range(H2 // P):
                    pe.wait_ge(s_h, done)
                    for k in range(H1 // P):
                        mm = pe.matmul(h2_ps[nb], wt2[:, k, nb * P:(nb + 1) * P], h1T[:, k, :],
                                       start=(k == 0), stop=(k == H1 // P - 1))
                    mm.then_inc(s_h_ps, 1)
                done += H2 // P
                pe.wait_ge(s_h, done)
                for k in range(H2 // P):
                    mm = pe.matmul(cur0_ps[0:1, :], wt3[:, k:k + 1], h2T[:, k, :],
                                   start=(k == 0), stop=(k == H2 // P - 1))
                mm.then_inc(s_h_ps, 1)
                done += 1

        @block.scalar
        def _(act):
            def cur0_hi_part(q, hi):
                cols = slice(LO, COLS) if hi else slice(0, LO)
                if hi:
                    act.wait_ge(s_cross0, q + 1)
                else:
                    act.wait_ge(s_cur0, BLOCKS * (q + 1))
                act.activation(cur0_hi[:, cols], cur0_ps[:, cols], ACT.Copy).then_inc(s_cur0_hi, 1)

            def copy_gram(n):
                act.wait_ge(s_gram_ps, n + 1)
                at = (n * CHUNK_B) % (2 * P)
                act.activation(gram[:, :, bass.ds(at, CHUNK_B)].rearrange("p f b -> p b f"),
                               gram_ps[:, 0:CHUNK_B * FP].rearrange("p (b f) -> p b f", f=FP),
                               ACT.Copy).then_inc(s_gram, 1)

            def group(q, pos, first):
                c, j = divmod(pos, GROUPS)
                n = QUAD * q + c
                act.wait_ge(s_y, POSITIONS * q + pos + 1)
                if j == ACT_GROUPS[0] and not (first and c < 2):
                    act.wait_ge(s_fold, 3 * (n - 2) + 1)
                for k in range(GROUP_F[j]):
                    f = GF * j + k
                    act.activation(scaled[:, c % 2, ACT_GROUPS.index(j), k * M:(k + 1) * M],
                                   y_ps[:, pos % Y_BANKS, k * M:(k + 1) * M], ACT.Copy,
                                   scale=x_act[:, c, f:f + 1]).then_inc(s_scaled, 1)

            def quad(q, first=False, last=False):
                if not first:
                    act.wait_ge(s_scaled, QUAD * ACT_F * q)
                act.wait_ge(s_x, 16 * (q + 1))
                act.activation(x_act[:, :, :], x_next[:, :, :], ACT.Copy).then_inc(s_x_act, 1)
                act.wait_ge(s_x_act, q + 1)
                for pos in range(POSITIONS):
                    if pos % GROUPS in ACT_GROUPS:
                        group(q, pos, first)
                    if pos == ACT_CUR0_HI:
                        cur0_hi_part(q, True)
                    if not last:
                        if pos == ACT_CUR0_LO:
                            cur0_hi_part(q + 1, False)
                    c, j = divmod(pos, GROUPS)
                    if j == ACT_GRAM and not (first and c < 2):
                        copy_gram(QUAD * q + c - 2)

            def cross12(t):
                act.wait_ge(s_out2_ps, t + 1)
                act.activation(cross1T[:, bass.ds(t * P, P)], gram[:, NF, bass.ds((t % 2) * P, P)],
                               ACT.Copy).then_inc(s_mlp_in, 1)
                act.activation(cross2T[:, bass.ds(t * P, P)], out2_ps[:, 0:P],
                               ACT.Copy).then_inc(s_mlp_in, 1)

            act.dma_start(ident[:, :], identity).then_inc(s_ident_in, 16)
            act.dma_start(pair_stage, w0_pair.rearrange("j p m -> p j m")).then_inc(s_w0_in, 16)
            act.dma_start(twin_stage, w0_twin.rearrange("j p m -> p j m")).then_inc(s_w0_in, 16)
            act.dma_start(f1_stage.rearrange("g (f m) -> g f m", m=M),
                          f1.rearrange("(f g) m -> g f m", g=M)).then_inc(s_f1_in, 16)
            act.wait_ge(s_zeroD, 2)
            act.dma_start(dense_sb[:, :, 0:DENSE], dense.rearrange("(t p) k -> p t k", p=P)).then_inc(s_dense_in, 16)
            act.dma_start(wt1[:, 0:3, :], w_top1[0:3 * M, :].rearrange("(k p) n -> p k n", p=P)).then_inc(s_rest_in, 16)
            act.dma_start(wt1[0:DENSE, 3, :], w_top1[3 * M:3 * M + DENSE, :]).then_inc(s_rest_in, 16)
            act.dma_start(w2_sb[:, :].rearrange("g (f m) -> g f m", m=M),
                          f2.rearrange("(f g) m -> g f m", g=M)).then_inc(s_rest_in, 16)
            act.dma_start(wt2[:, :, :], w_top2.rearrange("(k p) n -> p k n", p=P)).then_inc(s_rest_in, 16)
            act.dma_start(wt3[:, :], w_top3.rearrange("(k p) a -> p (k a)", p=P),
                          allow_slow_non_contiguous=True).then_inc(s_rest_in, 16)
            act.dma_start(bt1[:, :], b_top1.rearrange("(k p) -> p k", p=P),
                          allow_slow_non_contiguous=True).then_inc(s_rest_in, 16)
            act.dma_start(bt2[:, :], b_top2.rearrange("(k p) -> p k", p=P),
                          allow_slow_non_contiguous=True).then_inc(s_rest_in, 16)

            act.wait_ge(s_f1_in, 16)
            act.activation(w1_hi[:, :], f1_stage, ACT.Copy).then_inc(s_w1_hi, 1)
            act.wait_ge(s_dT_ps, 1)
            for i in range(2):
                act.activation(denseT[:, i * 512:(i + 1) * 512], y_ps[:, i, :], ACT.Copy).then_inc(s_mlp_in, 1)

            cur0_hi_part(0, False)
            quad(0, first=True)
            with act.Fori(0, TILES - 1) as t:
                with act.Fori(0, TILE_QUADS) as i:
                    quad(t * TILE_QUADS + i + 1)
                cross12(t)
            with act.Fori(QUADS - TILE_QUADS + 1, QUADS - 1) as q:
                quad(q)
            quad(QUADS - 1, last=True)
            copy_gram(CHUNKS - 2)
            copy_gram(CHUNKS - 1)
            cross12(TILES - 1)

            act.wait_ge(s_rest_in, 16 * 7)
            done = 0
            for half in range(2):
                for mb in range(H1 // P):
                    done += 1
                    act.wait_ge(s_h_ps, done)
                    act.activation(h1T[:, mb, :], y_ps[:, mb, :], ACT.Relu, bias=bt1[:, mb:mb + 1]).then_inc(s_h, 1)
                for nb in range(H2 // P):
                    done += 1
                    act.wait_ge(s_h_ps, done)
                    act.activation(h2T[:, nb, :], h2_ps[nb], ACT.Relu, bias=bt2[:, nb:nb + 1]).then_inc(s_h, 1)
                done += 1
                act.wait_ge(s_h_ps, done)
                act.activation(y_sb[:, half * 512:(half + 1) * 512], cur0_ps[0:1, :], ACT.Copy).then_inc(s_h, 1)

        @block.vector
        def _(dve):
            def make_pairs(q, j, first):
                if j == 0:
                    dve.wait_ge(s_shift0, 16 * BLOCK_SHIFTS * (q + 1))
                    dve.wait_ge(s_shift1, 16 * 2 * BLOCK_SHIFTS * (q + 1))
                if j >= SLOTS:
                    dve.wait_ge(s_cur0, BLOCKS * q + j - SLOTS + 1)
                elif not first:
                    dve.wait_ge(s_cur0, BLOCKS * q)
                dve.tensor_tensor(pairs[:, j % SLOTS, :], x_shift[:, j, :], x_rep[:, :], ALU.mult).then_inc(s_pairs, 1)

            def cur0_lo_part(q, hi):
                cols = slice(LO, COLS) if hi else slice(0, LO)
                dve.wait_ge(s_cur0_hi, 2 * q + (2 if hi else 1))
                dve.tensor_tensor(cur0_lo[:, cols], cur0_ps[:, cols], cur0_hi[:, cols].bitcast(F32),
                                  ALU.subtract).then_inc(s_cur0_lo, 1)

            def sum_cross0(q):
                dve.tensor_reduce(cross0T[:, bass.ds(q * QUAD_B, QUAD_B)],
                                  cur0_ps[:, :].rearrange("p (b d) -> p b d", d=D), AX.X, ALU.add).then_inc(s_cross0, 1)

            def group(q, pos, first):
                c, j = divmod(pos, GROUPS)
                if j == 0 and not (first and c < 2):
                    dve.wait_ge(s_fold, 3 * (QUAD * q + c - 2) + 2)
                dve.wait_ge(s_y, POSITIONS * q + pos + 1)
                for k in range(GF):
                    f = GF * j + k
                    y = y_ps[:, pos % Y_BANKS, k * M:(k + 1) * M]
                    a = acc[:, c % 2, (k % 2) * M:(k % 2 + 1) * M]
                    x = x_dve[:, c, f:f + 1]
                    if j == 0 and k < 2:
                        dve.tensor_scalar(a, y, x, None, ALU.mult).then_inc(s_acc, 1)
                    else:
                        dve.wait_ge(s_acc, q * (QUAD * DVE_F) + c * DVE_F + taken(DVE_GROUPS, j - 1) + k - 1)
                        dve.scalar_tensor_tensor(out=a, in0=y, scalar=x, in1=a, op0=ALU.mult,
                                                 op1=ALU.add).then_inc(s_acc, 1)

            def fold_chunk(n, par, step, first):
                if step == 0:
                    dve.wait_ge(s_added, ADDS * (n + 1))
                    dve.tensor_tensor(fold[:, 0, :], scaled[:, par, 0, 0:2 * M], scaled[:, par, 0, 2 * M:4 * M],
                                      ALU.add).then_inc(s_fold, 1)
                if step == 1:
                    dve.wait_ge(s_fold, 3 * n + 1)
                    dve.tensor_tensor(fold[:, 1, :], fold[:, 0, :], acc[:, par, :], ALU.add).then_inc(s_fold, 1)
                if step == 2:
                    if not first:
                        dve.wait_ge(s_gram_ps, n - 1)
                    dve.wait_ge(s_fold, 3 * n + 2)
                    dve.tensor_tensor(cur1[:, par, :], fold[:, 1, 0:M], fold[:, 1, M:2 * M], ALU.add).then_inc(s_fold, 1)

            def quad(q, first=False, last=False):
                if not first:
                    dve.wait_ge(s_acc, QUAD * DVE_F * q)
                dve.wait_ge(s_x, 16 * (q + 1))
                dve.tensor_copy(x_dve[:, :, :], x_next[:, :, :]).then_inc(s_x_dve, 1)
                dve.wait_ge(s_x_dve, q + 1)
                for pos in range(POSITIONS):
                    if pos % GROUPS in DVE_GROUPS:
                        group(q, pos, first)
                    if pos == DVE_CUR0_HI:
                        cur0_lo_part(q, True)
                    if not last:
                        if pos in DVE_PAIRS:
                            make_pairs(q + 1, DVE_PAIRS.index(pos), False)
                        if pos == DVE_CUR0_LO:
                            cur0_lo_part(q + 1, False)
                        if pos == DVE_CROSS0:
                            sum_cross0(q + 1)
                    c, j = divmod(pos, GROUPS)
                    if j in DVE_FOLD and not (first and c == 0):
                        fold_chunk(QUAD * q + c - 1, (c - 1) % 2, DVE_FOLD.index(j), first and c < 3)

            dve.memset(dense_sb[:, :, :], 0.0).then_inc(s_zeroD, 1)
            dve.memset(wt1[:, 3, :], 0.0).then_inc(s_zeroD, 1)
            dve.memset(x_rep[:, :], 0.0).then_inc(s_zeroD, 1)
            dve.memset(x_shift[:, :, :], 0.0).then_inc(s_zeroD, 1)
            dve.wait_ge(s_w0_in, 32)
            dve.tensor_tensor(w0_sym[:, :, :], pair_stage, twin_stage, ALU.add).then_inc(s_w0, 1)
            dve.wait_ge(s_w1_hi, 1)
            dve.tensor_tensor(w1_lo[:, :], f1_stage, w1_hi[:, :].bitcast(F32), ALU.subtract).then_inc(s_w1_lo, 1)

            for j in range(BLOCKS):
                make_pairs(0, j, True)
            cur0_lo_part(0, False)
            sum_cross0(0)
            quad(0, first=True)
            with dve.Fori(1, QUADS - 1) as q:
                quad(q)
            quad(QUADS - 1, last=True)
            for step in range(3):
                fold_chunk(CHUNKS - 1, (CHUNKS - 1) % 2, step, False)


def kernel(**inputs):
    import concourse.bacc as bacc
    from concourse.bass_utils import run_bass_kernel_spmd

    nc = bacc.Bacc("TRN2", target_bir_lowering=False, num_devices=1)
    arrays = {}

    def arg(name, a):
        a = np.ascontiguousarray(a)
        arrays[f"in_{name}"] = a
        return nc.dram_tensor(f"in_{name}", a.shape, mybir.dt.from_np(a.dtype), kind="ExternalInput").ap()

    f0 = np.asarray(inputs["L0_rec_f0"]).reshape(NF, NF, M)
    w0_pair = np.zeros((BLOCKS, P, M), f0.dtype)
    w0_twin = np.zeros((BLOCKS, P, M), f0.dtype)
    for s in range(SHIFTS):
        j, r = divmod(s, BLOCK_SHIFTS)
        for f in range(NF):
            g = (f + s) % NF
            row = r * NF + f
            w0_pair[j, row] = f0[f, g]
            if s:
                w0_twin[j, row] = f0[g, f]

    args = dict(
        dense=arg("dense", inputs["dense_ctx"]),
        ids=arg("ids", inputs["ids"]),
        tables=[arg(f"tbl_{f}", inputs[f"tbl_{f}"]) for f in range(NF)],
        w_top1=arg("w_top1", inputs["W_top1"]),
        b_top1=arg("b_top1", inputs["b_top1"]),
        w_top2=arg("w_top2", inputs["W_top2"]),
        b_top2=arg("b_top2", inputs["b_top2"]),
        w_top3=arg("w_top3", inputs["W_top3"]),
        w0_pair=arg("w0_pair", w0_pair),
        w0_twin=arg("w0_twin", w0_twin),
        f1=arg("f1", inputs["L0_rec_f1"]),
        f2=arg("f2", inputs["L0_rec_f2"]),
        identity=arg("identity", np.eye(P, dtype=np.float32)),
    )
    out = nc.dram_tensor("out_y", (BATCH, 1), F32, kind="ExternalOutput").ap()
    build(nc, out=out, **args)
    r = run_bass_kernel_spmd(nc, [arrays], core_ids=[0])
    return r.results[0]["out_y"]
```

```python
from contextlib import ExitStack

import numpy as np

import concourse.bass as bass
from concourse import mybir

F32 = mybir.dt.float32
F32R = mybir.dt.float32r
I32 = mybir.dt.int32
U32 = mybir.dt.uint32
ALU = mybir.AluOpType
ACT = mybir.ActivationFunctionType
AX = mybir.AxisListType

BATCH = 1024
NF = 39
D = 16
M = 128
DENSE = 16
H1, H2 = 512, 256

P = 128
FP = NF + 1
CHUNK_B = P // D
QUAD = 4
COLS = QUAD * P
QUAD_B = QUAD * CHUNK_B
QUADS = BATCH // QUAD_B
TILES = BATCH // P
TILE_QUADS = QUADS // TILES
TILE_CHUNKS = TILE_QUADS * QUAD
CHUNKS = QUADS * QUAD

SHIFTS = (NF + 1) // 2
BLOCK_SHIFTS = 3
BLOCKS = -(-SHIFTS // BLOCK_SHIFTS)

GF = 4
GROUPS = -(-NF // GF)
GROUP_F = [min(GF, NF - GF * j) for j in range(GROUPS)]
POSITIONS = QUAD * GROUPS
DVE_GROUPS = [0, 3, 5, 8]
ACT_GROUPS = [j for j in range(GROUPS) if j not in DVE_GROUPS]
DVE_F = sum(GROUP_F[j] for j in DVE_GROUPS)
ACT_F = sum(GROUP_F[j] for j in ACT_GROUPS)
ADDS = len(ACT_GROUPS) - 2
LAST = len(ACT_GROUPS) - 1
FOLDS = 5
Y_BANKS = 5
assert GROUPS % Y_BANKS == 0 and all(GROUP_F[j] == GF for j in range(GROUPS - 1))
assert ACT_GROUPS[-1] == GROUPS - 1 and GROUP_F[-1] == GF - 1

DVE_PAIRS = [1, 3, 9, 13, 15, 22, 24]
ACT_PAIRS_HI = [2, 6, 9, 15, 16, 24, 26]
DVE_PAIRS_LO = [4, 6, 12, 15, 16, 25, 30]
PE_W0 = [9, 12, 16, 21, 24, 30, 34]
ACT_CUR0_LO, ACT_CUR0_HI = 33, 0
DVE_CUR0_LO, DVE_CROSS0, DVE_CUR0_HI = 34, 37, 3
PE_GRAM = 5
ACT_GRAM = 4
DVE_FOLD = [2, 3, 5, 6, 8]
L2_SHARES, L2_SHARES_END = [11, 11, 11, 6], [15, 15, 9]
L2_SPAN = 21
ACT_CROSS12 = 24
X_LOADS = 1 + CHUNK_B
LO = 3 * P
PAIR_SLOTS = 2
SLOTS = 3
FIRST_HALF = 4
GATHERED_AT = 9
EARLY_F = BLOCKS * BLOCK_SHIFTS - 1

DENSE_AT = (0, 32, 64)
DENSE_ROWS = 96


def taken(groups, pos):
    c, last = divmod(pos, GROUPS)
    return c * sum(GROUP_F[j] for j in groups) + sum(GROUP_F[j] for j in groups if j <= last)


def shares(sizes):
    return [range(sum(sizes[:i]), sum(sizes[:i + 1])) for i in range(len(sizes))]


def build(nc, dense, ids, tables, w_top1, b_top1, w_top2, b_top2, w_top3, w0_pair, w0_twin, f1, f2,
          identity, out):
    scratch = nc.dram_tensor("x0_by_column", [BATCH * D, FP], F32, kind="Internal").ap()
    scratch_tiles = scratch.rearrange("(b d) f -> b (d f)", d=D)
    scratch_chunks = scratch.rearrange("(n p) f -> p n f", p=P)

    rows = NF + BLOCKS * BLOCK_SHIFTS - 1
    scratchT = nc.dram_tensor("x0_by_feature", [rows, BATCH * D], F32, kind="Internal").ap()
    scratchT_samples = scratchT.rearrange("f (b d) -> b f d", d=D)

    with ExitStack() as ctx:
        def sb(name, shape, dt=F32):
            return ctx.enter_context(nc.sbuf_tensor(name, shape, dt))

        def psum(name, shape):
            return ctx.enter_context(nc.psum_tensor(name, shape, F32))

        def sem(name):
            return ctx.enter_context(nc.semaphore(name))

        w1_hi = sb("w1_hi", [P, NF * M], F32R)
        w1_lo = sb("w1_lo", [P, NF * M], F32R)
        w2_sb = sb("w2_sb", [P, NF * M])
        w0_hi = sb("w0_hi", [P, BLOCKS, M], F32R)
        w0_lo = sb("w0_lo", [P, BLOCKS, M], F32R)
        ident = sb("ident", [P, P])
        w_dense = sb("w_dense", [P, H1], F32R)
        wt3 = sb("wt3", [P, H2 // P])
        bt1 = sb("bt1", [P, H1 // P])
        bt2 = sb("bt2", [P, H2 // P])
        ids_sb = sb("ids_sb", [P, NF], I32)
        gathered_x = sb("gathered_x", [P, NF, D])
        permuted_x = sb("permuted_x", [P, D, FP])
        x_sb = sb("x_sb", [P, 2, QUAD, FP])
        x_diag = sb("x_diag", [P, 2, QUAD, CHUNK_B * FP])
        x_rep = sb("x_rep", [P, COLS])
        x_shift = sb("x_shift", [P, BLOCKS, COLS])
        pairs = sb("pairs", [P, PAIR_SLOTS, COLS])
        pairs_hi = sb("pairs_hi", [P, SLOTS, COLS], F32R)
        pairs_lo = sb("pairs_lo", [P, SLOTS, COLS], F32R)
        cur0_hi = sb("cur0_hi", [P, COLS], F32R)
        cur0_lo = sb("cur0_lo", [P, COLS], F32R)
        scaled = sb("scaled", [P, 2, len(ACT_GROUPS), GF * M])
        acc = sb("acc", [P, 2, 2 * M])
        fold = sb("fold", [P, 2, 2 * M])
        cur1 = sb("cur1", [P, 2, M])
        gram = sb("gram", [P, FP, 2 * P])
        cross0T = sb("cross0T", [P, BATCH])
        cross1T = sb("cross1T", [P, BATCH])
        cross2T = sb("cross2T", [P, BATCH])
        denseT = sb("denseT", [P, BATCH], F32R)

        stage = gram[:, :, :].rearrange("p f b -> p (f b)")
        f1_stage = stage[:, 0:NF * M]
        o = NF * M
        pair_stage = stage[:, o:o + BLOCKS * M].rearrange("p (j m) -> p j m", m=M)
        o += BLOCKS * M
        twin_stage = stage[:, o:o + BLOCKS * M].rearrange("p (j m) -> p j m", m=M)
        o += BLOCKS * M
        dense_w_stage = stage[0:DENSE_ROWS, o:o + H1]
        dense_sb = scaled[:, 0, 0:2, 0:TILES // 2 * DENSE_ROWS].rearrange("p a (t k) -> p a t k", k=DENSE_ROWS)
        blocks1, blocks2 = H1 // P, H2 // P
        h1T = [x_shift[:, 0:blocks1, :], scaled[:, 0, 0:blocks1, :]]
        h2T = [x_shift[:, blocks1:blocks1 + blocks2, :], scaled[:, 1, 0:blocks2, :]]
        y_sb = [x_shift[0:1, blocks1 + blocks2, :], x_rep[0:1, :]]

        wt1 = gram[:, 0:3 * blocks1, 0:P].rearrange("p (k n) m -> p k n m", n=blocks1)
        wt2 = gram[:, 3 * blocks1:3 * blocks1 + blocks1 * blocks2, 0:P].rearrange(
            "p (k n) m -> p k n m", n=blocks2)

        y_ps = psum("y_ps", [P, Y_BANKS, 512])
        out2_ps = psum("out2_ps", [P, 512])
        cur0_ps = psum("cur0_ps", [P, 512])
        gram_ps = psum("gram_ps", [P, 512])

        h2_ps = [[y_ps[:, 4, :], out2_ps[:, :]], [y_ps[:, 0, :], y_ps[:, 1, :]]]
        result_ps = [cur0_ps[0:1, :], gram_ps[0:1, :]]

        s_ids = sem("s_ids")
        s_gathered_early = sem("s_gathered_early")
        s_gathered = sem("s_gathered")
        s_permuted = sem("s_permuted")
        s_scratch = sem("s_scratch")
        s_scratchT = sem("s_scratchT")
        s_first_quad = sem("s_first_quad")
        s_first_tile = sem("s_first_tile")
        s_shift0 = sem("s_shift0")
        s_rep = sem("s_rep")
        s_shift1 = sem("s_shift1")
        s_x = sem("s_x")
        s_ident_in = sem("s_ident_in")
        s_w0_in = sem("s_w0_in")
        s_f1_in = sem("s_f1_in")
        s_rest_in = sem("s_rest_in")
        s_mlp_w_in = sem("s_mlp_w_in")
        s_dense_in = sem("s_dense_in")
        s_out = sem("s_out")
        s_zero = sem("s_zero")
        s_zeroD = sem("s_zeroD")
        s_w0 = sem("s_w0")
        s_w0_hi = sem("s_w0_hi")
        s_w0_lo = sem("s_w0_lo")
        s_w1_hi = sem("s_w1_hi")
        s_w1_lo = sem("s_w1_lo")
        s_pairs = sem("s_pairs")
        s_pairs_hi = sem("s_pairs_hi")
        s_pairs_lo = sem("s_pairs_lo")
        s_cur0 = sem("s_cur0")
        s_cur0_hi = sem("s_cur0_hi")
        s_cur0_lo = sem("s_cur0_lo")
        s_cross0 = sem("s_cross0")
        s_y = sem("s_y")
        s_acc = sem("s_acc")
        s_scaled = sem("s_scaled")
        s_added = sem("s_added")
        s_fold = sem("s_fold")
        s_gram_ps = sem("s_gram_ps")
        s_gram = sem("s_gram")
        s_out2_ps = sem("s_out2_ps")
        s_mlp_in = sem("s_mlp_in")
        s_dT_ps = sem("s_dT_ps")
        s_dense_w_in = sem("s_dense_w_in")
        s_dense_hi = sem("s_dense_hi")
        s_dense_lo = sem("s_dense_lo")
        s_h_ps = sem("s_h_ps")
        s_h = sem("s_h")

        block = ctx.enter_context(nc.Block())

        @block.sync
        def _(sp):
            def load_ids(q):
                sp.dma_start(ids_sb[:, :], ids[bass.ds(q * QUAD_B, P), :]).then_inc(s_ids, 16)

            def load_x(q, par):
                sp.dma_start(x_sb[:, par, :, :],
                             scratch_chunks[:, bass.ds(q * QUAD, QUAD), :]).then_inc(s_x, 16)

            def load_diag(q, par):
                for k in range(CHUNK_B):
                    sp.dma_start(x_diag[k * D:(k + 1) * D, par, :, k * FP:(k + 1) * FP],
                                 scratch_chunks[k * D:(k + 1) * D, bass.ds(q * QUAD, QUAD), :]
                                 ).then_inc(s_x, 16)

            def load_shift(q, half):
                j0, j1 = (0, FIRST_HALF) if half == 0 else (FIRST_HALF, BLOCKS)
                for s in range(BLOCK_SHIFTS):
                    at = slice(s * NF, (s + 1) * NF)
                    source = bass.AP(tensor=scratchT.tensor, offset=(s + j0 * BLOCK_SHIFTS) * BATCH * D + q * COLS,
                                     ap=[[BATCH * D, NF], [BLOCK_SHIFTS * BATCH * D, j1 - j0], [1, COLS]])
                    sp.dma_start(x_shift[at, j0:j1, :], source).then_inc(s_shift1 if half else s_shift0, 16)

            def load_rep(q):
                for s in range(BLOCK_SHIFTS):
                    sp.dma_start(x_rep[s * NF:(s + 1) * NF, :],
                                 scratchT[0:NF, bass.ds(q * COLS, COLS)]).then_inc(s_rep, 16)

            def load_pair_factors(q, first):
                if not first:
                    sp.wait_ge(s_pairs, BLOCKS * (q - 1) + FIRST_HALF)
                load_shift(q, 0)
                if not first:
                    sp.wait_ge(s_pairs, BLOCKS * q)
                load_rep(q)
                if not first:
                    sp.wait_ge(s_x, 16 * X_LOADS * q)
                load_shift(q, 1)

            def load_quad(q, half, first, second):
                if not (first or second):
                    sp.wait_ge(s_cur0, BLOCKS * q + 1)
                load_x(q, half)
                if not (first or second):
                    sp.wait_ge(s_gram_ps, QUAD * (q - 1))
                load_diag(q, half)

            def write_by_feature(q0):
                sp.wait_ge(s_gathered, q0 * (16 * NF // TILE_QUADS) + 16 * (NF - EARLY_F))
                tile_rows = bass.ds(q0 * QUAD_B, P)
                sp.dma_start(scratchT_samples[tile_rows, 0:NF, :], gathered_x[:, :, :]).then_inc(s_scratchT, 16)
                sp.dma_start(scratchT_samples[tile_rows, NF:rows, :],
                             gathered_x[:, 0:EARLY_F, :]).then_inc(s_scratchT, 16)

            def write_first_by_feature():
                sp.wait_ge(s_gathered_early, 16 * EARLY_F)
                for row in (0, NF):
                    sp.dma_start(scratchT_samples[0:P, row:row + EARLY_F, :],
                                 gathered_x[:, 0:EARLY_F, :]).then_inc(s_scratchT, 16)
                sp.wait_ge(s_gathered, 16 * (NF - EARLY_F))
                for b0, b1, landed in ((0, QUAD_B, s_first_quad), (QUAD_B, P, s_first_tile)):
                    sp.dma_start(scratchT_samples[b0:b1, EARLY_F:NF, :],
                                 gathered_x[b0:b1, EARLY_F:NF, :]).then_inc(landed, 16)

            def write_by_column(q0):
                sp.wait_ge(s_permuted, q0 + TILE_QUADS)
                sp.dma_start(scratch_tiles[bass.ds(q0 * QUAD_B, P), :],
                             permuted_x[:, :, :].rearrange("p d f -> p (d f)")).then_inc(s_scratch, 16)

            def tile(q0, last):
                for i in range(TILE_QUADS):
                    q = q0 + i
                    if i == 0:
                        write_by_feature(q0)
                        write_by_column(q0)
                        if not last:
                            load_ids(q0 + TILE_QUADS)
                        sp.wait_ge(s_scratchT, q0 * (32 // TILE_QUADS) + 32)
                        sp.wait_ge(s_scratch, q0 * (16 // TILE_QUADS) + 16)
                    load_pair_factors(q, False)
                    load_quad(q, i % 2, False, False)

            load_ids(0)
            write_first_by_feature()
            write_by_column(0)
            sp.wait_ge(s_scratchT, 32)
            sp.wait_ge(s_first_quad, 16)
            sp.wait_ge(s_zeroD, 5)
            load_pair_factors(0, True)
            load_ids(TILE_QUADS)
            sp.wait_ge(s_scratch, 16)
            load_quad(0, 0, True, False)
            sp.wait_ge(s_first_tile, 16)
            for q in range(1, TILE_QUADS):
                load_pair_factors(q, False)
                load_quad(q, q % 2, False, q == 1)
            with sp.Fori(TILE_QUADS, QUADS - 2 * TILE_QUADS + 1, TILE_QUADS) as q0:
                tile(q0, False)
            tile(QUADS - TILE_QUADS, True)
            for half in range(2):
                sp.wait_ge(s_h, 2 * (blocks1 + blocks2) + half + 1)
                sp.dma_start(out[half * 512:(half + 1) * 512, :].rearrange("b a -> a b"),
                             y_sb[half]).then_inc(s_out, 16)
            sp.wait_ge(s_out, 32)

        @block.gpsimd
        def _(pool):
            def gather(f, landed=s_gathered):
                pool.indirect_dma_start(gathered_x[:, f, :], None, tables[f],
                                        bass.IndirectOffsetOnAxis(ids_sb[:, f:f + 1].bitcast(U32), 0)
                                        ).then_inc(landed, 16)

            def permute():
                pool.tensor_copy(permuted_x[:, :, 0:NF],
                                 gathered_x[:, :, :].rearrange("p f d -> p d f")).then_inc(s_permuted, TILE_QUADS)

            def add_chunk(n, par):
                for k in range(1, LAST):
                    pool.wait_ge(s_scaled, n * ACT_F + taken(ACT_GROUPS, ACT_GROUPS[k]))
                    if k > 1:
                        pool.wait_ge(s_added, n * ADDS + k - 1)
                    pool.tensor_tensor(scaled[:, par, 0, :], scaled[:, par, 0, :], scaled[:, par, k, :],
                                       ALU.add).then_inc(s_added, 1)

            def start_gathers(t, first=False):
                pool.wait_ge(s_ids, 16 * (t + 1))
                if first:
                    pool.wait_ge(s_first_quad, 16)
                    pool.wait_ge(s_first_tile, 16)
                pool.wait_ge(s_scratchT, 32 * t)

            share = [NF * i // TILE_CHUNKS for i in range(TILE_CHUNKS + 1)]
            early = TILE_CHUNKS - GATHERED_AT

            def tile(t, more):
                for c in range(TILE_CHUNKS):
                    if c == GATHERED_AT:
                        pool.wait_ge(s_gathered, 16 * NF * (t + 2) - 16 * EARLY_F)
                        pool.wait_ge(s_scratch, 16 * (t + 1))
                    if c == GATHERED_AT + 1 and more:
                        start_gathers(t + 2)
                    add_chunk(t * TILE_CHUNKS + c, c % 2)
                    if c < GATHERED_AT:
                        i = c + early
                        for f in range(share[i], share[i + 1]):
                            gather(f)
                    if c == GATHERED_AT:
                        permute()
                    if c > GATHERED_AT and more:
                        i = c - GATHERED_AT
                        for f in range(share[i - 1] if i > 1 else 0, share[i] if c < TILE_CHUNKS - 1 else share[early]):
                            gather(f)

            pool.memset(permuted_x[:, :, NF:FP], 1.0).then_inc(s_zero, 1)
            pool.wait_ge(s_ids, 16)
            for f in range(NF):
                gather(f, s_gathered_early if f < EARLY_F else s_gathered)
            pool.wait_ge(s_gathered_early, 16 * EARLY_F)
            pool.wait_ge(s_gathered, 16 * (NF - EARLY_F))
            pool.wait_ge(s_zero, 1)
            permute()
            start_gathers(1, True)
            for f in range(share[early]):
                gather(f)
            with pool.Fori(0, TILES - 2) as t:
                tile(t, True)
            tile(TILES - 2, False)
            with pool.Fori(0, TILE_CHUNKS // 2) as c2:
                for par in range(2):
                    add_chunk((TILES - 1) * TILE_CHUNKS + 2 * c2 + par, par)

        @block.tensor
        def _(pe):
            assert PE_W0[0] >= Y_BANKS

            def layer0(q, j, first):
                pe.wait_ge(s_pairs_lo, BLOCKS * q + j + 1)
                if j == 0 and not first:
                    pe.wait_ge(s_cur0_lo, 2 * q)
                hi, lo = pairs_hi[:, j % SLOTS, :], pairs_lo[:, j % SLOTS, :]
                pe.matmul(cur0_ps[:, :], w0_hi[:, j, :], hi, start=(j == 0), stop=False)
                pe.matmul(cur0_ps[:, :], w0_lo[:, j, :], hi, start=False, stop=False)
                pe.matmul(cur0_ps[:, :], w0_hi[:, j, :], lo, start=False,
                          stop=(j == BLOCKS - 1)).then_inc(s_cur0, 1)

            def gram_chunk(q, c, n, par, first):
                pe.wait_ge(s_fold, FOLDS * (n + 1))
                pe.wait_ge(s_x, 16 * X_LOADS * (q + 1))
                if not first:
                    pe.wait_ge(s_gram, n)
                pe.matmul(gram_ps[:, 0:CHUNK_B * FP], cur1[:, c % 2, :],
                          x_diag[:, bass.ds(par, 1), c, :].rearrange("p a n -> p (a n)"),
                          start=True, stop=True).then_inc(s_gram_ps, 1)

            def bank_read(q, pos):
                if pos % GROUPS in DVE_GROUPS:
                    pe.wait_ge(s_acc, q * (QUAD * DVE_F) + taken(DVE_GROUPS, pos))
                else:
                    pe.wait_ge(s_scaled, q * (QUAD * ACT_F) + taken(ACT_GROUPS, pos))

            def group(q, pos, first):
                c, j = divmod(pos, GROUPS)
                w = M * GROUP_F[j]
                if not (first and pos < Y_BANKS):
                    bank_read(q, pos - Y_BANKS)
                if pos == 0:
                    pe.wait_ge(s_cur0_lo, 2 * q + 1)
                if pos == 3 * GROUPS:
                    pe.wait_ge(s_cur0_lo, 2 * q + 2)
                y = y_ps[:, pos % Y_BANKS, 0:w]
                ws = slice(j * GF * M, j * GF * M + w)
                xs = slice(c * P, (c + 1) * P)
                pe.matmul(y, cur0_hi[:, xs], w1_hi[:, ws], start=True, stop=False)
                pe.matmul(y, cur0_hi[:, xs], w1_lo[:, ws], start=False, stop=False)
                pe.matmul(y, cur0_lo[:, xs], w1_hi[:, ws], start=False, stop=True).then_inc(s_y, 1)

            def quad(q, first=False, last=False, t=None, features=(), span=POSITIONS):
                for pos in range(POSITIONS):
                    group(q, pos, first)
                    for k, f in enumerate(features):
                        if pos == span * k // len(features):
                            layer2(t, f)
                    if not last:
                        if pos in PE_W0:
                            layer0(q + 1, PE_W0.index(pos), False)
                    c, j = divmod(pos, GROUPS)
                    if j == PE_GRAM and not (first and c < 2):
                        behind = 1 if c < 2 else 0
                        gram_chunk(q - behind, (c - 2) % QUAD, QUAD * q + c - 2, (q - behind) % 2, first and c == 2)

            def layer2(t, f):
                if f == 0:
                    pe.wait_ge(s_gram, TILE_CHUNKS * (t + 1))
                mm = pe.matmul(out2_ps[:, 0:P], w2_sb[:, f * M:(f + 1) * M],
                               gram[:, f, bass.ds((t % 2) * P, P)], start=(f == 0), stop=(f == NF - 1))
                if f == NF - 1:
                    mm.then_inc(s_out2_ps, 1)

            pe.wait_ge(s_ident_in, 16)
            pe.wait_ge(s_dense_in, 16 * 6)
            for t in range(TILES):
                mm = pe.transpose(y_ps[0:DENSE_ROWS, t // 4, (t % 4) * P:(t % 4 + 1) * P],
                                  dense_sb[:, t // 4, t % 4, :], ident[:, :])
            mm.then_inc(s_dT_ps, 1)
            pe.wait_ge(s_w0_lo, 1)
            for j in range(BLOCKS):
                layer0(0, j, True)
            pe.wait_ge(s_w1_lo, 1)
            pe.wait_ge(s_dense_lo, 2)

            quad(0, first=True)
            pe.wait_ge(s_rest_in, 16 * 4)
            with pe.Fori(1, TILE_QUADS + 1) as q:
                quad(q)
            with pe.Fori(1, TILES - 1) as t:
                for i, features in enumerate(shares(L2_SHARES)):
                    quad(t * TILE_QUADS + i + 1, t=t - 1, features=features,
                         span=L2_SPAN if i == TILE_QUADS - 1 else POSITIONS)
            for i, features in enumerate(shares(L2_SHARES_END)):
                at_end = i == TILE_QUADS - 2
                quad(QUADS - TILE_QUADS + i + 1, last=at_end, t=TILES - 2, features=features,
                     span=L2_SPAN if at_end else POSITIONS)

            def hidden1(half, mb):
                cols = slice(half * 512, half * 512 + 512)
                pe.matmul(y_ps[:, mb, :], w_dense[0:DENSE_ROWS, mb * P:(mb + 1) * P], denseT[0:DENSE_ROWS, cols],
                          start=True, stop=False)
                for k, src in enumerate((cross0T, cross1T, cross2T)):
                    if half and mb == 0 and k == 1:
                        pe.wait_ge(s_mlp_in, 2 * TILES)
                    mm = pe.matmul(y_ps[:, mb, :], wt1[:, k, mb, :], src[:, cols], start=False, stop=(k == 2))
                mm.then_inc(s_h_ps, 1)

            pe.wait_ge(s_mlp_w_in, 16 * (3 + blocks1))
            pe.wait_ge(s_mlp_in, 2 * (TILES - 1))
            for mb in range(blocks1):
                if mb == blocks1 - 1:
                    for c in (QUAD - 2, QUAD - 1):
                        gram_chunk(QUADS - 1, c, CHUNKS - QUAD + c, (QUADS - 1) % 2, False)
                bank_read(QUADS - 1, POSITIONS - Y_BANKS + mb)
                hidden1(0, mb)
            for f in range(NF):
                layer2(TILES - 1, f)
            for mb in range(blocks1):
                pe.wait_ge(s_h, mb + 1)
                hidden1(1, mb)
            for half in range(2):
                for nb in range(blocks2):
                    pe.wait_ge(s_h, blocks1 * (half + 1))
                    for k in range(blocks1):
                        mm = pe.matmul(h2_ps[half][nb], wt2[:, k, nb, :], h1T[half][:, k, :],
                                       start=(k == 0), stop=(k == blocks1 - 1))
                    mm.then_inc(s_h_ps, 1)
            for half in range(2):
                pe.wait_ge(s_h, 2 * blocks1 + blocks2 * (half + 1))
                for k in range(blocks2):
                    mm = pe.matmul(result_ps[half], wt3[:, k:k + 1], h2T[half][:, k, :],
                                   start=(k == 0), stop=(k == blocks2 - 1))
                mm.then_inc(s_h_ps, 1)

        @block.scalar
        def _(act):
            def cur0_hi_part(q, hi):
                cols = slice(LO, COLS) if hi else slice(0, LO)
                if hi:
                    act.wait_ge(s_cross0, q + 1)
                else:
                    act.wait_ge(s_cur0, BLOCKS * (q + 1))
                act.activation(cur0_hi[:, cols], cur0_ps[:, cols], ACT.Copy).then_inc(s_cur0_hi, 1)

            def pairs_hi_part(q, j, first):
                act.wait_ge(s_pairs, BLOCKS * q + j + 1)
                if not (first and j < SLOTS):
                    act.wait_ge(s_cur0, BLOCKS * q + max(j - SLOTS + 1, 0))
                act.activation(pairs_hi[:, j % SLOTS, :], pairs[:, j % PAIR_SLOTS, :], ACT.Copy).then_inc(s_pairs_hi, 1)

            def copy_gram(n):
                act.wait_ge(s_gram_ps, n + 1)
                at = (n * CHUNK_B) % (2 * P)
                act.activation(gram[:, :, bass.ds(at, CHUNK_B)].rearrange("p f b -> p b f"),
                               gram_ps[:, 0:CHUNK_B * FP].rearrange("p (b f) -> p b f", f=FP),
                               ACT.Copy).then_inc(s_gram, 1)

            def group(q, par, pos, first):
                c, j = divmod(pos, GROUPS)
                n = QUAD * q + c
                act.wait_ge(s_y, POSITIONS * q + pos + 1)
                if j == ACT_GROUPS[0] and not (first and c < 2):
                    act.wait_ge(s_fold, FOLDS * (n - 1))
                for k in range(GROUP_F[j]):
                    f = GF * j + k
                    act.activation(scaled[:, c % 2, ACT_GROUPS.index(j), k * M:(k + 1) * M],
                                   y_ps[:, pos % Y_BANKS, k * M:(k + 1) * M], ACT.Copy,
                                   scale=x_sb[:, par, c, f:f + 1]).then_inc(s_scaled, 1)

            def quad(q, par, first=False, last=False, t=None):
                act.wait_ge(s_x, 16 * X_LOADS * (q + 1))
                for pos in range(POSITIONS):
                    if pos % GROUPS in ACT_GROUPS:
                        group(q, par, pos, first)
                    if pos == ACT_CUR0_HI:
                        cur0_hi_part(q, True)
                    if not last:
                        if pos in ACT_PAIRS_HI:
                            pairs_hi_part(q + 1, ACT_PAIRS_HI.index(pos), False)
                        if pos == ACT_CUR0_LO:
                            cur0_hi_part(q + 1, False)
                    c, j = divmod(pos, GROUPS)
                    if pos == ACT_CROSS12 and t is not None:
                        cross12(t)
                        if last:
                            load_mlp_weights()
                    if j == ACT_GRAM and not (first and c < 2):
                        if c == 2 and t is not None:
                            act.wait_ge(s_mlp_in, 2 * t + 2)
                        copy_gram(QUAD * q + c - 2)

            def cross12(t):
                act.wait_ge(s_out2_ps, t + 1)
                act.activation(cross1T[:, bass.ds(t * P, P)], gram[:, NF, bass.ds((t % 2) * P, P)],
                               ACT.Copy).then_inc(s_mlp_in, 1)
                act.activation(cross2T[:, bass.ds(t * P, P)], out2_ps[:, 0:P],
                               ACT.Copy).then_inc(s_mlp_in, 1)

            def load_mlp_weights():
                act.wait_ge(s_mlp_in, 2 * (TILES - 1))
                for k in range(3):
                    act.dma_start(wt1[:, k, :, :], w_top1[k * P:(k + 1) * P, :].rearrange(
                        "p (n m) -> p n m", m=P)).then_inc(s_mlp_w_in, 16)
                for k in range(blocks1):
                    act.dma_start(wt2[:, k, :, :], w_top2[k * P:(k + 1) * P, :].rearrange(
                        "p (n m) -> p n m", m=P)).then_inc(s_mlp_w_in, 16)

            act.dma_start(ident[:, :], identity).then_inc(s_ident_in, 16)
            act.dma_start(pair_stage, w0_pair.rearrange("j p m -> p j m")).then_inc(s_w0_in, 16)
            act.dma_start(twin_stage, w0_twin.rearrange("j p m -> p j m")).then_inc(s_w0_in, 16)
            act.dma_start(f1_stage.rearrange("g (f m) -> g f m", m=M),
                          f1.rearrange("(f g) m -> g f m", g=M)).then_inc(s_f1_in, 16)
            act.wait_ge(s_zeroD, 2)
            dense_tiles = dense.rearrange("(a t p) k -> p a t k", p=P, t=TILES // 2)
            for at in DENSE_AT:
                for a in range(2):
                    act.dma_start(dense_sb[:, a, :, at:at + DENSE], dense_tiles[:, a, :, :]).then_inc(s_dense_in, 16)
                act.dma_start(dense_w_stage[at:at + DENSE, :],
                              w_top1[3 * M:3 * M + DENSE, :]).then_inc(s_dense_w_in, 16)
            act.dma_start(w2_sb[:, :].rearrange("g (f m) -> g f m", m=M),
                          f2.rearrange("(f g) m -> g f m", g=M)).then_inc(s_rest_in, 16)
            act.dma_start(wt3[:, :], w_top3.rearrange("(k p) a -> p (k a)", p=P),
                          allow_slow_non_contiguous=True).then_inc(s_rest_in, 16)
            act.dma_start(bt1[:, :], b_top1.rearrange("(k p) -> p k", p=P),
                          allow_slow_non_contiguous=True).then_inc(s_rest_in, 16)
            act.dma_start(bt2[:, :], b_top2.rearrange("(k p) -> p k", p=P),
                          allow_slow_non_contiguous=True).then_inc(s_rest_in, 16)

            act.wait_ge(s_w0, 1)
            act.activation(w0_hi[:, :, :], pair_stage, ACT.Copy).then_inc(s_w0_hi, 1)
            act.wait_ge(s_f1_in, 16)
            act.activation(w1_hi[:, :], f1_stage, ACT.Copy).then_inc(s_w1_hi, 1)
            act.wait_ge(s_dT_ps, 1)
            for i in range(2):
                act.activation(denseT[0:DENSE_ROWS, i * 512:(i + 1) * 512], y_ps[0:DENSE_ROWS, i, :],
                               ACT.Copy).then_inc(s_dense_hi, 1)
            act.wait_ge(s_dense_w_in, 16 * 3)
            act.activation(w_dense[0:DENSE_ROWS, :], dense_w_stage, ACT.Copy).then_inc(s_dense_hi, 1)

            for j in range(BLOCKS):
                pairs_hi_part(0, j, True)
            cur0_hi_part(0, False)
            quad(0, 0, first=True)
            with act.Fori(1, TILE_QUADS, 2) as q:
                quad(q, 1)
                quad(q + 1, 0)
            with act.Fori(1, TILES - 1) as t:
                for i in range(TILE_QUADS):
                    quad(t * TILE_QUADS + i + 1, (i + 1) % 2, t=t - 1 if i == TILE_QUADS - 1 else None)
            for q in range(QUADS - TILE_QUADS + 1, QUADS):
                last = q == QUADS - 1
                quad(q, q % 2, last=last, t=TILES - 2 if last else None)

            def relu(done, to, source, bias):
                act.wait_ge(s_h_ps, done + 1)
                act.activation(to, source, ACT.Relu, bias=bias).then_inc(s_h, 1)

            act.wait_ge(s_rest_in, 16 * 4)
            for mb in range(blocks1):
                if mb == blocks1 - 1:
                    copy_gram(CHUNKS - 2)
                    copy_gram(CHUNKS - 1)
                relu(mb, h1T[0][:, mb, :], y_ps[:, mb, :], bt1[:, mb:mb + 1])
            cross12(TILES - 1)
            for mb in range(blocks1):
                relu(blocks1 + mb, h1T[1][:, mb, :], y_ps[:, mb, :], bt1[:, mb:mb + 1])
            for half in range(2):
                for nb in range(blocks2):
                    relu(2 * blocks1 + half * blocks2 + nb, h2T[half][:, nb, :], h2_ps[half][nb], bt2[:, nb:nb + 1])
            for half in range(2):
                act.wait_ge(s_h_ps, 2 * (blocks1 + blocks2) + half + 1)
                act.activation(y_sb[half], result_ps[half], ACT.Copy).then_inc(s_h, 1)

        @block.vector
        def _(dve):
            def make_pairs(q, j, first):
                if j == 0:
                    dve.wait_ge(s_shift0, 16 * BLOCK_SHIFTS * (q + 1))
                    dve.wait_ge(s_rep, 16 * BLOCK_SHIFTS * (q + 1))
                if j == FIRST_HALF:
                    dve.wait_ge(s_shift1, 16 * BLOCK_SHIFTS * (q + 1))
                if not (first and j < PAIR_SLOTS):
                    dve.wait_ge(s_pairs_lo, BLOCKS * q + max(j - PAIR_SLOTS + 1, 0))
                dve.tensor_tensor(pairs[:, j % PAIR_SLOTS, :], x_shift[:, j, :], x_rep[:, :],
                                  ALU.mult).then_inc(s_pairs, 1)

            def pairs_lo_part(q, j):
                dve.wait_ge(s_pairs_hi, BLOCKS * q + j + 1)
                dve.tensor_tensor(pairs_lo[:, j % SLOTS, :], pairs[:, j % PAIR_SLOTS, :],
                                  pairs_hi[:, j % SLOTS, :].bitcast(F32), ALU.subtract).then_inc(s_pairs_lo, 1)

            def cur0_lo_part(q, hi):
                cols = slice(LO, COLS) if hi else slice(0, LO)
                dve.wait_ge(s_cur0_hi, 2 * q + (2 if hi else 1))
                dve.tensor_tensor(cur0_lo[:, cols], cur0_ps[:, cols], cur0_hi[:, cols].bitcast(F32),
                                  ALU.subtract).then_inc(s_cur0_lo, 1)

            def sum_cross0(q):
                dve.tensor_reduce(cross0T[:, bass.ds(q * QUAD_B, QUAD_B)],
                                  cur0_ps[:, :].rearrange("p (b d) -> p b d", d=D), AX.X, ALU.add).then_inc(s_cross0, 1)

            def group(q, par, pos, first):
                c, j = divmod(pos, GROUPS)
                if j == 0 and not (first and c < 2):
                    dve.wait_ge(s_fold, FOLDS * (QUAD * q + c - 2) + 1)
                dve.wait_ge(s_y, POSITIONS * q + pos + 1)
                for k in range(GF):
                    f = GF * j + k
                    y = y_ps[:, pos % Y_BANKS, k * M:(k + 1) * M]
                    a = acc[:, c % 2, (k % 2) * M:(k % 2 + 1) * M]
                    x = x_sb[:, par, c, f:f + 1]
                    if j == 0 and k < 2:
                        dve.tensor_scalar(a, y, x, None, ALU.mult).then_inc(s_acc, 1)
                    else:
                        dve.wait_ge(s_acc, q * (QUAD * DVE_F) + c * DVE_F + taken(DVE_GROUPS, j - 1) + k - 1)
                        dve.scalar_tensor_tensor(out=a, in0=y, scalar=x, in1=a, op0=ALU.mult,
                                                 op1=ALU.add).then_inc(s_acc, 1)

            def fold_chunk(n, par, step, first):
                last_group = scaled[:, par, LAST, :]
                if not (first and n == 0 and step == 0):
                    dve.wait_ge(s_fold, FOLDS * n + step)
                if step == 0:
                    dve.wait_ge(s_scaled, ACT_F * (n + 1))
                    dve.tensor_tensor(fold[:, 0, :], last_group[:, 0:2 * M], acc[:, par, :], ALU.add).then_inc(s_fold, 1)
                if step == 1:
                    dve.wait_ge(s_added, ADDS * (n + 1))
                    dve.tensor_tensor(fold[:, 1, :], scaled[:, par, 0, 0:2 * M], scaled[:, par, 0, 2 * M:4 * M],
                                      ALU.add).then_inc(s_fold, 1)
                if step == 2:
                    dve.tensor_tensor(fold[:, 0, :], fold[:, 0, :], fold[:, 1, :], ALU.add).then_inc(s_fold, 1)
                if step == 3:
                    dve.tensor_tensor(fold[:, 1, 0:M], fold[:, 0, 0:M], fold[:, 0, M:2 * M], ALU.add).then_inc(s_fold, 1)
                if step == 4:
                    if not first:
                        dve.wait_ge(s_gram_ps, n - 1)
                    dve.tensor_tensor(cur1[:, par, :], fold[:, 1, 0:M], last_group[:, 2 * M:3 * M],
                                      ALU.add).then_inc(s_fold, 1)

            def quad(q, par, first=False, last=False):
                dve.wait_ge(s_x, 16 * X_LOADS * (q + 1))
                for pos in range(POSITIONS):
                    if pos % GROUPS in DVE_GROUPS:
                        group(q, par, pos, first)
                    if pos == DVE_CUR0_HI:
                        cur0_lo_part(q, True)
                    if not last:
                        if pos in DVE_PAIRS:
                            make_pairs(q + 1, DVE_PAIRS.index(pos), False)
                        if pos in DVE_PAIRS_LO:
                            pairs_lo_part(q + 1, DVE_PAIRS_LO.index(pos))
                        if pos == DVE_CUR0_LO:
                            cur0_lo_part(q + 1, False)
                        if pos == DVE_CROSS0:
                            sum_cross0(q + 1)
                    c, j = divmod(pos, GROUPS)
                    if j in DVE_FOLD and not (first and c == 0):
                        fold_chunk(QUAD * q + c - 1, (c - 1) % 2, DVE_FOLD.index(j), first and c < 3)

            dve.memset(dense_sb, 0.0).then_inc(s_zeroD, 1)
            dve.memset(dense_w_stage, 0.0).then_inc(s_zeroD, 1)
            dve.memset(x_rep[:, :], 0.0).then_inc(s_zeroD, 1)
            dve.memset(x_shift[:, :, :], 0.0).then_inc(s_zeroD, 1)
            dve.memset(x_diag[:, :, :, :], 0.0).then_inc(s_zeroD, 1)
            dve.wait_ge(s_w0_in, 32)
            dve.tensor_tensor(pair_stage, pair_stage, twin_stage, ALU.add).then_inc(s_w0, 1)
            dve.wait_ge(s_w0_hi, 1)
            dve.tensor_tensor(w0_lo[:, :, :], pair_stage, w0_hi[:, :, :].bitcast(F32), ALU.subtract).then_inc(s_w0_lo, 1)
            dve.wait_ge(s_w1_hi, 1)
            dve.tensor_tensor(w1_lo[:, :], f1_stage, w1_hi[:, :].bitcast(F32), ALU.subtract).then_inc(s_w1_lo, 1)

            rows = slice(DENSE_AT[2], DENSE_ROWS)
            for i in range(2):
                dve.wait_ge(s_dense_hi, i + 1)
                part = denseT[rows, i * 512:(i + 1) * 512]
                dve.tensor_tensor(part, y_ps[rows, i, :], part.bitcast(F32), ALU.subtract).then_inc(s_dense_lo, 1)
            rows = slice(DENSE_AT[1], DENSE_AT[2])
            dve.wait_ge(s_dense_hi, 3)
            dve.tensor_tensor(w_dense[rows, :], dense_w_stage[rows, :], w_dense[rows, :].bitcast(F32),
                              ALU.subtract).then_inc(s_dense_lo, 1)

            for j in range(BLOCKS):
                make_pairs(0, j, True)
                if j:
                    pairs_lo_part(0, j - 1)
            pairs_lo_part(0, BLOCKS - 1)
            cur0_lo_part(0, False)
            sum_cross0(0)
            quad(0, 0, first=True)
            with dve.Fori(1, QUADS - 2, 2) as q:
                quad(q, 1)
                quad(q + 1, 0)
            quad(QUADS - 1, 1, last=True)
            for step in range(FOLDS):
                fold_chunk(CHUNKS - 1, (CHUNKS - 1) % 2, step, False)


def kernel(**inputs):
    import concourse.bacc as bacc
    from concourse.bass_utils import run_bass_kernel_spmd

    nc = bacc.Bacc("TRN2", target_bir_lowering=False, num_devices=1)
    arrays = {}

    def arg(name, a):
        a = np.ascontiguousarray(a)
        arrays[f"in_{name}"] = a
        return nc.dram_tensor(f"in_{name}", a.shape, mybir.dt.from_np(a.dtype), kind="ExternalInput").ap()

    f0 = np.asarray(inputs["L0_rec_f0"]).reshape(NF, NF, M)
    w0_pair = np.zeros((BLOCKS, P, M), f0.dtype)
    w0_twin = np.zeros((BLOCKS, P, M), f0.dtype)
    for s in range(SHIFTS):
        j, r = divmod(s, BLOCK_SHIFTS)
        for f in range(NF):
            g = (f + s) % NF
            row = r * NF + f
            w0_pair[j, row] = f0[f, g]
            if s:
                w0_twin[j, row] = f0[g, f]

    args = dict(
        dense=arg("dense", inputs["dense_ctx"]),
        ids=arg("ids", inputs["ids"]),
        tables=[arg(f"tbl_{f}", inputs[f"tbl_{f}"]) for f in range(NF)],
        w_top1=arg("w_top1", inputs["W_top1"]),
        b_top1=arg("b_top1", inputs["b_top1"]),
        w_top2=arg("w_top2", inputs["W_top2"]),
        b_top2=arg("b_top2", inputs["b_top2"]),
        w_top3=arg("w_top3", inputs["W_top3"]),
        w0_pair=arg("w0_pair", w0_pair),
        w0_twin=arg("w0_twin", w0_twin),
        f1=arg("f1", inputs["L0_rec_f1"]),
        f2=arg("f2", inputs["L0_rec_f2"]),
        identity=arg("identity", np.eye(P, dtype=np.float32)),
    )
    out = nc.dram_tensor("out_y", (BATCH, 1), F32, kind="ExternalOutput").ap()
    build(nc, out=out, **args)
    r = run_bass_kernel_spmd(nc, [arrays], core_ids=[0])
    return r.results[0]["out_y"]
```
